# Optimizing a Trainium2 kernel written in Bass

```python
import numpy as np
import jax
import jax.numpy as jnp

def _softmax(x, axis=-1):
    return jax.nn.softmax(x, axis=axis)

def _gelu(x):
    return jax.nn.gelu(x, approximate=True)

def _silu(x):
    return jax.nn.silu(x)

def _sigmoid(x):
    return jax.nn.sigmoid(x)

def _layernorm(x, axis=-1, eps=1e-05):
    m = jnp.mean(x, axis=axis, keepdims=True)
    v = jnp.var(x, axis=axis, keepdims=True)
    return (x - m) / jnp.sqrt(v + eps)

def _scatter_add(tgt, idx, src, axis=0):
    return tgt.at[idx].add(src)

def _segment_sum(src, seg, n):
    return jax.ops.segment_sum(src, seg, n)
kernel_name = 'mk_conv_seq_d2_conv_nchw256_r4_ece2c6'

def setup_inputs(seed: int=0):
    np.random.seed(seed)
    _w = jnp.asarray

    def _rec_inputs():
        import jax
        import jax.numpy as jnp
        _gk = jax.random.key(seed)
        x = -0.000125 + 0.9999 * jax.random.normal(jax.random.fold_in(_gk, 1), (32, 64, 16, 16), jnp.float32)
        return x
    x = _rec_inputs()

    def _L0_conv_setup():
        import jax, jax.numpy as jnp
        from jax import lax
        import numpy as np
        key = jax.random.key(seed)
        k1, k2, k3 = jax.random.split(key, 3)
        B, C, H, W = (32, 64, 16, 16)
        KC, KS = (5, 5)
        x = jax.random.normal(k1, (B, C, H, W), dtype=jnp.float32)
        w_c = jax.random.normal(k2, (1, 1, KC), dtype=jnp.float32) * 0.3
        w_s = jax.random.normal(k3, (1, 2, KS, KS), dtype=jnp.float32) * 0.2
        return {'x': x, 'w_c': w_c, 'w_s': w_s}
    _L0_conv_all = _L0_conv_setup()
    _L0_conv_in = {k: v for k, v in _L0_conv_all.items() if k in ('w_c', 'w_s')}
    del _L0_conv_all

    def _L1_conv_setup():
        import math
        import jax, jax.numpy as jnp
        import numpy as np
        CHANNELS = 64
        NUM_HEADS = 4
        GROUPS = 32
        EPS = 1e-05
        key = jax.random.key(seed)
        ks = jax.random.split(key, 7)
        b, c, h, w = (8, CHANNELS, 48, 48)
        return {'x': jax.random.normal(ks[0], (b, c, h, w), dtype=jnp.float32), 'gn_w': jax.random.uniform(ks[1], (c,), dtype=jnp.float32), 'gn_b': jax.random.normal(ks[2], (c,), dtype=jnp.float32) * 0.02, 'qkv_w': jax.random.normal(ks[3], (3 * c, c), dtype=jnp.float32) * (1.0 / math.sqrt(c)), 'qkv_b': jax.random.normal(ks[4], (3 * c,), dtype=jnp.float32) * 0.02, 'proj_w': jax.random.normal(ks[5], (c, c), dtype=jnp.float32) * (1.0 / math.sqrt(c)), 'proj_b': jax.random.normal(ks[6], (c,), dtype=jnp.float32) * 0.02}
    _L1_conv_all = _L1_conv_setup()
    _L1_conv_in = {k: v for k, v in _L1_conv_all.items() if k in ('gn_w', 'gn_b', 'qkv_w', 'qkv_b', 'proj_w', 'proj_b')}
    del _L1_conv_all
    return {'x': x, 'L0_conv_w_c': _L0_conv_in['w_c'], 'L0_conv_w_s': _L0_conv_in['w_s'], 'L1_conv_gn_w': _L1_conv_in['gn_w'], 'L1_conv_gn_b': _L1_conv_in['gn_b'], 'L1_conv_qkv_w': _L1_conv_in['qkv_w'], 'L1_conv_qkv_b': _L1_conv_in['qkv_b'], 'L1_conv_proj_w': _L1_conv_in['proj_w'], 'L1_conv_proj_b': _L1_conv_in['proj_b']}

def reference(x, L0_conv_w_c, L0_conv_w_s, L1_conv_gn_w, L1_conv_gn_b, L1_conv_qkv_w, L1_conv_qkv_b, L1_conv_proj_w, L1_conv_proj_b):
    import jax
    import jax.numpy as jnp

    def _L0_conv_ref(x, w_c, w_s):
        import jax, jax.numpy as jnp
        from jax import lax
        import numpy as np
        y = jnp.mean(x, axis=(2, 3))
        y = lax.conv_general_dilated(y[:, None, :], w_c, (1,), 'SAME')[:, 0, :]
        yc = jax.nn.sigmoid(x * y[:, :, None, None])
        avg_out = jnp.mean(yc, axis=1, keepdims=True)
        max_out = jnp.max(yc, axis=1, keepdims=True)
        sa_in = jnp.concatenate([avg_out, max_out], axis=1)
        sa = jax.nn.sigmoid(lax.conv_general_dilated(sa_in, w_s, (1, 1), 'SAME'))
        return yc * sa + x

    def _L1_conv_ref(x, gn_w, gn_b, qkv_w, qkv_b, proj_w, proj_b):
        import math
        import jax, jax.numpy as jnp
        import numpy as np
        CHANNELS = 64
        NUM_HEADS = 4
        GROUPS = 32
        EPS = 1e-05
        b, c, h, w = x.shape
        nh = NUM_HEADS
        hd = c // nh
        hw = h * w
        xg = x.reshape(b, GROUPS, c // GROUPS, h, w)
        mean = jnp.mean(xg, axis=(2, 3, 4), keepdims=True)
        var = jnp.mean(jnp.square(xg - mean), axis=(2, 3, 4), keepdims=True)
        xn = (xg - mean) * jax.lax.rsqrt(var + EPS)
        xn = xn.reshape(b, c, h, w) * gn_w[None, :, None, None] + gn_b[None, :, None, None]
        qkv = jnp.einsum('bchw,oc->bohw', xn, qkv_w) + qkv_b[None, :, None, None]
        q, k, v = jnp.split(qkv, 3, axis=1)
        q = q.reshape(b, nh, hd, hw)
        k = k.reshape(b, nh, hd, hw)
        v = v.reshape(b, nh, hd, hw)
        scale = 1.0 / math.sqrt(hd)
        attn = jnp.einsum('bndi,bndj->bnij', q, k) * scale
        attn = jax.nn.softmax(attn, axis=-1)
        out = jnp.einsum('bnij,bndj->bndi', attn, v)
        out = out.reshape(b, c, h, w)
        out = jnp.einsum('bchw,oc->bohw', out, proj_w) + proj_b[None, :, None, None]
        return x + out

    def _gn(v, G=32, eps=1e-05):
        B_, C_, H_, W_ = v.shape
        g = v.reshape(B_, G, C_ // G, H_, W_)
        m = jnp.mean(g, axis=(2, 3, 4), keepdims=True)
        s = jnp.var(g, axis=(2, 3, 4), keepdims=True)
        return ((g - m) / jnp.sqrt(s + eps)).reshape(v.shape)

    def _ln_c(v, eps=1e-06):
        m = jnp.mean(v, axis=1, keepdims=True)
        s = jnp.var(v, axis=1, keepdims=True)
        return (v - m) / jnp.sqrt(s + eps)

    def _ln_t(v, eps=1e-05):
        m = jnp.mean(v, axis=-1, keepdims=True)
        s = jnp.var(v, axis=-1, keepdims=True)
        return (v - m) / jnp.sqrt(s + eps)

    def _to_tokens(v):
        B_, C_, H_, W_ = v.shape
        return v.reshape(B_, C_, H_ * W_).transpose(0, 2, 1)

    def _from_tokens(t, like):
        B_, C_, H_, W_ = like.shape
        return t.transpose(0, 2, 1).reshape(B_, C_, H_, W_)
    x = _L0_conv_ref(x, L0_conv_w_c, L0_conv_w_s)
    x = _L1_conv_ref(x, L1_conv_gn_w, L1_conv_gn_b, L1_conv_qkv_w, L1_conv_qkv_b, L1_conv_proj_w, L1_conv_proj_b)
    return x

_drawn_inputs = setup_inputs


def setup_inputs(seed=0):
    import zlib

    import numpy as np

    out = dict(_drawn_inputs(seed))
    spreads = {}
    factors = {'L0_conv_w_c': 6.445,
     'L0_conv_w_s': 15.909,
     'L1_conv_gn_b': 2.963,
     'L1_conv_qkv_b': 3.23,
     'L1_conv_proj_b': 2.797}
    for name, (base, spread) in spreads.items():
        noise = np.random.default_rng([zlib.crc32(name.encode()), seed]).standard_normal(out[name].shape)
        drawn = base * np.exp(spread * noise) if base else spread * noise
        out[name] = jnp.asarray(drawn.astype(out[name].dtype))
    for name, factor in factors.items():
        out[name] = (out[name] * factor).astype(out[name].dtype)
    return out
```

```python
from contextlib import ExitStack

import concourse.bass as bass
from concourse import mybir

F32 = mybir.dt.float32
BF16 = mybir.dt.bfloat16
ALU = mybir.AluOpType
ACT = mybir.ActivationFunctionType
AX = mybir.AxisListType

P = 128
IMAGES, C, SIDE = 32, 64, 16
N = SIDE * SIDE
PAIRS = IMAGES // 2
HEADS, HD = 4, 16
TILES = N // P
KS = 5
GROUP = 4
GROUPS = PAIRS // GROUP
SLOTS = 6
KQ = SLOTS * HD
UNITS = 2 * HEADS
RING = 3
EPS = 1e-5
GN = 8
SCALE = float(HD) ** -0.5
KPAD = SIDE * (SIDE + KS - 1)

C_IDENT, C_BAND, C_DX, C_GROUP, C_MEAN = 0, 128, 768, 848, 976
C_END = 978


def program(nc, x, w_rows, vecs, w_all, consts, out):
    ctx = ExitStack()
    with ctx:
        def sb(name, shape, dt=F32):
            return ctx.enter_context(nc.sbuf_tensor(name, shape, dt))

        def sem(name):
            return ctx.enter_context(nc.semaphore(name))

        bank = [ctx.enter_context(nc.psum_tensor(f"bank{i}", [P, 512], F32)) for i in range(8)]
        parts_dram = nc.dram_tensor("parts_dram", [RING, 3, 2, HD, HEADS * 2 * N], BF16).ap()
        gate_dram = nc.dram_tensor("gate_dram", [IMAGES, N], F32).ap()

        xall = sb("xall", [P, PAIRS, N])
        ycall = sb("ycall", [P, PAIRS, N])
        gate = sb("gate", [P, PAIRS, N])
        con = sb("con", [P, C_END])
        wall = sb("wall", [P, 448])
        vec = sb("vec", [P, 5])
        wrow = sb("wrow", [P, KS + 2 * KS * KS])
        ident = con[:, C_IDENT:C_IDENT + P]
        groupavg = con[:, C_GROUP:C_GROUP + P]
        identb = sb("identb", [P, P], BF16)
        ysum = sb("ysum", [P, PAIRS])
        ytap = sb("ytap", [P, GROUPS, KS, GROUP])
        yscale = sb("yscale", [P, PAIRS])
        bandprod = sb("bandprod", [P, 2 * KS * SIDE * KS])
        bandrow = sb("bandrow", [P, 2, KS * SIDE])
        toep = sb("toep", [P, 2, TILES, KPAD])
        maps = sb("maps", [P, TILES, 2, IMAGES])
        gate_s = sb("gate_s", [IMAGES, N])
        pbias = sb("pbias", [P, 1])
        bn6 = sb("bn6", [P, 6])
        mv = sb("mv", [P, 2])
        gmv = sb("gmv", [P, 2])
        negvar = sb("negvar", [P, 1])
        vareps = sb("vareps", [P, 1])
        gna = sb("gna", [P, 1])
        gnb = sb("gnb", [P, 1])
        xn = sb("xn", [P, RING, N])
        z32 = sb("z32", [P, 2 * N])
        rest = sb("rest", [P, 2 * N])
        parts = sb("parts", [P, RING, 3, 2 * N], BF16)
        qs = sb("qs", [P, RING, HEADS, 2, N], BF16)
        ks = sb("ks", [P, RING, HEADS, 2, N], BF16)
        negmax = sb("negmax", [P, RING, HEADS, 2, TILES], BF16)
        maxrow = sb("maxrow", [16, RING, P], BF16)
        pt = sb("pt", [P, UNITS, TILES, N])
        vs = sb("vs", [P, RING, TILES, 2, HEADS, 2 * HD])
        rstd = sb("rstd", [P, 1])
        mhalf = sb("mhalf", [P, 1])
        otok = sb("otok", [P, 2 * N // 32, 32])
        orec = sb("orec", [P, 2 * N // 32])
        onorm = sb("onorm", [P, 2 * N])
        yo = sb("yo", [P, RING, N])
        outb = sb("outb", [P, RING, N])

        b_qk, b_v, b_p, w_gn, b_gn = (vec[:, i:i + 1] for i in range(5))
        w_qk = [wall[:, a * P:(a + 1) * P] for a in range(2)]
        w_v = wall[:, 256:384]
        w_p = wall[:, 384:448]

        s_bank = [bank[0], bank[1]]
        st_bank = [bank[2], bank[3]]
        o_bank = bank[4]
        z_bank = bank[5]
        v_psum = bank[6][:, 0:256]
        mt_psum = bank[6][0:16, 320:384].bitcast(BF16)
        y_psum = bank[7][:, 0:256]
        gs_psum = bank[7][:, 0:2]

        rows_in, con_in, wall_in, vec_in = sem("rows_in"), sem("con_in"), sem("wall_in"), sem("vec_in")
        x_in = [sem(f"x_in{g}") for g in range(GROUPS)]
        mhalf_ready = sem("mhalf_ready")
        identb_ready, fixed_ready = sem("identb_ready"), sem("fixed_ready")
        ysum_ready, ytap_ready, yconv_ready, ys_ready = sem("ysum_ready"), sem("ytap_ready"), sem("yconv_ready"), sem("ys_ready")
        yc_ready, yt_ready, cmax_done, avg_ready, maps_ready = sem("yc_ready"), sem("yt_ready"), sem("cmax_done"), sem("avg_ready"), sem("maps_ready")
        prod_ready, band_ready, toep_zero, toep_in = sem("prod_ready"), sem("band_ready"), sem("toep_zero"), sem("toep_in")
        sconv_ready, gate_ready, gate_out = sem("sconv_ready"), sem("gate_ready"), sem("gate_out")
        gate_in = [sem(f"gate_in{g}") for g in range(GROUPS)]
        pb_ready, pbias_ready = sem("pb_ready"), sem("pbias_ready")

        u_ready, x1_ready = sem("u_ready"), sem("x1_ready")
        gn_step = sem("gn_step")
        gs_ready, xn_ready = sem("gs_ready"), sem("xn_ready")
        z_ready, v_ready = sem("z_ready"), sem("v_ready")
        p1_ready, z32_ready = sem("p1_ready"), sem("z32_ready")
        split_step = sem("split_step")
        parts_out, stack_in = sem("parts_out"), [sem(f"stack_in{r}") for r in range(RING)]
        s_ready, max_done = sem("s_ready"), sem("max_done")
        mt_ready, mrow_ready, mrow_in = sem("mt_ready"), sem("mrow_ready"), sem("mrow_in")
        st_ready, exp_done = sem("st_ready"), sem("exp_done")
        vs_ready, pv_done = sem("vs_ready"), sem("pv_done")
        norm_step, y_ready = sem("norm_step"), sem("y_ready")
        rstd_ready = sem("rstd_ready")
        yo_ready, out_ready = sem("yo_ready"), sem("out_ready")
        stored = [sem(f"stored{r}") for r in range(RING)]

        def wait(eng, semaphore, value):
            if not isinstance(value, int) or value > 0:
                eng.wait_ge(semaphore, value)

        def at(t, p):
            return t[:, p, :] if isinstance(p, int) else t[:, bass.ds(p, 1), :].rearrange("p a n -> p (a n)")

        AHEAD = 4
        LOOP_FROM, LOOP_TO = 3, 12

        def pipeline(eng, turn):
            def peeled(turns):
                for k in turns:
                    turn(k, lambda d, k=k: (k + d) % RING, lambda d, k=k: 0 <= k + d < PAIRS,
                         lambda d, k=k: (k + d) // RING + 1)
            peeled(range(-AHEAD, LOOP_FROM))
            with eng.Fori(LOOP_FROM // RING, LOOP_TO // RING, 1) as laps:
                for j in range(RING):
                    turn(laps * RING + j, lambda d, j=j: (j + d) % RING, lambda d: True,
                         lambda d, j=j: laps + ((j + d) // RING + 1))
            peeled(range(LOOP_TO, PAIRS + 1))

        block = ctx.enter_context(nc.Block())

        @block.sync
        def _(sp):
            sp.dma_start(xall[:, 0:GROUP, :], x[0:2 * GROUP].rearrange("(g i) c n -> (i c) g n", i=2)).then_inc(x_in[0], 16)
            sp.dma_start(wrow[:, :], w_rows.partition_broadcast(P)).then_inc(rows_in, 16)
            sp.dma_start(con[:, :], consts).then_inc(con_in, 16)
            for g in range(1, GROUPS):
                sp.dma_start(xall[:, g * GROUP:(g + 1) * GROUP, :],
                             x[2 * g * GROUP:2 * (g + 1) * GROUP].rearrange("(g i) c n -> (i c) g n", i=2)).then_inc(x_in[g], 16)
            sp.wait_ge(toep_zero, 1)
            sp.wait_ge(band_ready, 1)
            for t in range(TILES):
                for y in range(SIDE // TILES):
                    r = slice(SIDE * y, SIDE * (y + 1))
                    col = (SIDE // TILES * t + y) * SIDE
                    sp.dma_start(toep[r, :, t, col:col + KS * SIDE], bandrow[r, :, :]).then_inc(toep_in, 16)
            sp.dma_start(wall[:, :], w_all).then_inc(wall_in, 16)
            sp.dma_start(vec[:, :], vecs).then_inc(vec_in, 16)
            sp.wait_ge(gate_ready, 1)
            sp.dma_start(gate_dram, gate_s[:, :]).then_inc(gate_out, 16)
            sp.wait_ge(gate_out, 16)
            for g in range(GROUPS):
                for a in range(2):
                    src = gate_dram[2 * g * GROUP:2 * (g + 1) * GROUP, :].rearrange("(q i) n -> i q n", i=2)[a]
                    sp.dma_start(gate[C * a:C * (a + 1), g * GROUP:(g + 1) * GROUP, :],
                                 src.unsqueeze(0).broadcast_to([C, GROUP, N])).then_inc(gate_in[g], 16)

            def turn(k, slot, has, lap):
                if has(2):
                    r = slot(2)
                    wait(sp, parts_out, 16 * (k + 3))
                    for first, q_parts, k_parts in ((0, (0, 1, 2), (0, 0, 0)), (3, (0, 1), (1, 1)), (5, (0,), (2,))):
                        m = len(q_parts)
                        rows = slice(first * HD, (first + m) * HD)
                        src_q = parts_dram[r, 0:m, 0, :, :].rearrange("s d n -> d s n")
                        src_k = parts_dram[r, k_parts[0], 1, :, :].unsqueeze(1).broadcast_to([HD, m, HEADS * 2 * N])
                        sp.dma_start(qs[rows, r, :, :, :].rearrange("p h a n -> p (h a n)"), src_q).then_inc(stack_in[r], 16)
                        sp.dma_start(ks[rows, r, :, :, :].rearrange("p h a n -> p (h a n)"), src_k).then_inc(stack_in[r], 16)
                if has(-1):
                    wait(sp, out_ready, k)
                    if isinstance(k, int):
                        dst = out[2 * (k - 1):2 * k].rearrange("i c n -> (i c) n")
                    else:
                        dst = out[bass.ds(2 * (k - 1), 2)].rearrange("i c n -> (i c) n")
                    sp.dma_start(dst, outb[:, slot(-1), :]).then_inc(stored[slot(-1)], 16)
                if has(1):
                    wait(sp, mrow_ready, k + 2)
                    sp.dma_start(qs[KQ:KQ + 1, slot(1), :, :, :].rearrange("p h a (t n) -> p (h a t) n", t=TILES),
                                 maxrow[:, slot(1), :]).then_inc(mrow_in, 16)
                if has(3):
                    r = slot(3)
                    wait(sp, split_step, 3 * (k + 4))
                    sp.dma_start(parts_dram[r].rearrange("s g d (h n) -> (g d h) s n", h=HEADS), parts[:, r, :, :]).then_inc(parts_out, 16)
            pipeline(sp, turn)
            for r in range(RING):
                sp.wait_ge(stored[r], 16 * len(range(r, PAIRS, RING)))

        @block.gpsimd
        def _(pool):
            nc.gpsimd.memset(toep[:, :, :, :], 0.0).then_inc(toep_zero, 1)
            nc.gpsimd.memset(mhalf[:, :], -0.5).then_inc(mhalf_ready, 1)
            pool.wait_ge(mhalf_ready, 1)
            nc.gpsimd.memset(vs[:, :, :, :, :, :].rearrange("p r t a h d -> p (r t a h) d")[:, :, HD:2 * HD], 1.0).then_inc(fixed_ready, 1)
            pool.wait_ge(fixed_ready, 1)
            nc.gpsimd.memset(ks[KQ:KQ + 1, :, :, :, :], 1.0).then_inc(fixed_ready, 1)

            pool.wait_ge(fixed_ready, 2)

            def turn(k, slot, has, lap):
                if has(-1):
                    wait(pool, yo_ready, k)
                    wait(pool, stored[slot(-1)], (lap(-1) - 1) * 16)
                    nc.gpsimd.tensor_tensor(outb[:, slot(-1), :], yo[:, slot(-1), :], at(xall, k - 1), ALU.add).then_inc(out_ready, 1)
                r = slot(3)
                if has(3):
                    wait(pool, p1_ready, k + 4)
                    wait(pool, z32_ready, k + 4)
                    nc.gpsimd.tensor_tensor(rest[:, :], z32[:, :], parts[:, r, 0, :], ALU.subtract).then_inc(split_step, 1)
                    wait(pool, split_step, 3 * (k + 3) + 1)
                if has(4):
                    for g in [(k + 4) // GROUP] if isinstance(k, int) else range(1, GROUPS):
                        pool.wait_ge(gate_in[g], 32)
                    nc.gpsimd.tensor_tensor(at(ycall, k + 4), at(ycall, k + 4), at(gate, k + 4), ALU.mult).then_inc(u_ready, 1)
                if has(3):
                    nc.gpsimd.tensor_scalar(parts[:, r, 1, :], rest[:, :], 1.0, 0.0, ALU.mult, ALU.add).then_inc(split_step, 1)
                if has(4):
                    pool.wait_ge(u_ready, k + 5)
                    nc.gpsimd.tensor_tensor(at(xall, k + 4), at(ycall, k + 4), at(xall, k + 4), ALU.add).then_inc(x1_ready, 1)
                if has(3):
                    wait(pool, split_step, 3 * (k + 3) + 2)
                    nc.gpsimd.tensor_tensor(parts[:, r, 2, :], rest[:, :], parts[:, r, 1, :], ALU.subtract).then_inc(split_step, 1)
                if has(4):
                    wait(pool, gn_step, GN * (k + 4) + 6)
                    nc.gpsimd.tensor_tensor(rstd[:, :], vareps[:, :], mhalf[:, :], ALU.pow).then_inc(rstd_ready, 1)
            pipeline(pool, turn)

        @block.scalar
        def _(act):
            act.wait_ge(con_in, 16)
            nc.scalar.copy(identb[:, :], ident).then_inc(identb_ready, 1)
            for g in range(GROUPS):
                act.wait_ge(yconv_ready, g + 1)
                nc.scalar.activation(yscale[:, g * GROUP:(g + 1) * GROUP], bank[2][:, g * GROUP:(g + 1) * GROUP],
                                     ACT.Copy, scale=1.0 / N).then_inc(ys_ready, 1)
                act.wait_ge(ys_ready, g + 1)
                for p in range(g * GROUP, (g + 1) * GROUP):
                    nc.scalar.activation(ycall[:, p, :], xall[:, p, :], ACT.Sigmoid,
                                         scale=yscale[:, p:p + 1]).then_inc(yc_ready, 1)
            act.wait_ge(sconv_ready, 1)
            nc.scalar.activation(gate_s[:, :], bank[4][0:IMAGES, 0:N], ACT.Sigmoid).then_inc(gate_ready, 1)

            def turn(k, slot, has, lap):
                def exps(u0, u1):
                    for u in range(u0, u1):
                        wait(act, st_ready, UNITS * k + u + 1)
                        if u % HEADS == 0:
                            wait(act, pv_done, 2 * (k - 1) + u // HEADS + 1)
                        nc.scalar.activation(pt[:, u, :, :].rearrange("p t n -> p (t n)"), st_bank[u % 2][:, :], ACT.Exp,
                                             scale=SCALE).then_inc(exp_done, 1)
                if has(0):
                    exps(0, 4)
                if has(3):
                    wait(act, z_ready, k + 4)
                    wait(act, parts_out, 16 * (k + 1))
                    nc.scalar.activation(parts[:, slot(3), 0, :], z_bank[:, :], ACT.Identity, bias=b_qk).then_inc(p1_ready, 1)
                    wait(act, split_step, 3 * (k + 2) + 1)
                    nc.scalar.activation(z32[:, :], z_bank[:, :], ACT.Identity, bias=b_qk).then_inc(z32_ready, 1)
                if has(0):
                    exps(4, 6)
                if has(1):
                    wait(act, v_ready, k + 2)
                    wait(act, pv_done, 2 * (k - 1))
                    nc.scalar.copy(vs[:, slot(1), :, :, :, :].rearrange("p t a h d -> p (t a h) d")[:, :, 0:HD],
                                   v_psum.rearrange("p (g d) -> p g d", d=HD)).then_inc(vs_ready, 1)
                if has(-1):
                    wait(act, y_ready, k)
                    nc.scalar.activation(yo[:, slot(-1), :], y_psum, ACT.Identity, bias=pbias[:, 0:1]).then_inc(yo_ready, 1)
                if has(0):
                    exps(6, 8)
                if has(1):
                    wait(act, mt_ready, k + 2)
                    wait(act, mrow_in, 16 * (k - 1))
                    nc.scalar.copy(maxrow[:, slot(1), :], mt_psum).then_inc(mrow_ready, 1)
            act.wait_ge(pbias_ready, 1)
            pipeline(act, turn)

        @block.vector
        def _(dve):
            def ysums(g):
                dve.wait_ge(x_in[g], 16)
                nc.vector.tensor_reduce(ysum[:, g * GROUP:(g + 1) * GROUP], xall[:, g * GROUP:(g + 1) * GROUP, :],
                                        AX.X, ALU.add).then_inc(ysum_ready, 1)
                dve.wait_ge(ysum_ready, g + 1)
                dve.wait_ge(rows_in, 16)
                taps = wrow[:, 0:KS].unsqueeze(2).broadcast_to([P, KS, GROUP])
                sums = ysum[:, g * GROUP:(g + 1) * GROUP].unsqueeze(1).broadcast_to([P, KS, GROUP])
                nc.vector.tensor_tensor(ytap[:, g, :, :], taps, sums, ALU.mult).then_inc(ytap_ready, 1)

            ysums(0)
            dve.wait_ge(con_in, 16)
            rows = 2 * KS
            dx_mask = con[:, C_DX:C_DX + SIDE * KS].rearrange("p (x d) -> p x d", d=KS).unsqueeze(1).broadcast_to([P, rows, SIDE, KS])
            dx_w = wrow[:, KS:KS + rows * KS].rearrange("p (r d) -> p r d", d=KS).unsqueeze(2).broadcast_to([P, rows, SIDE, KS])
            nc.vector.tensor_tensor(bandprod[:, :].rearrange("p (r x d) -> p r x d", r=rows, d=KS), dx_mask, dx_w,
                                    ALU.mult).then_inc(prod_ready, 1)
            dve.wait_ge(prod_ready, 1)
            nc.vector.tensor_reduce(bandrow[:, :, :].rearrange("p m n -> p (m n)"),
                                    bandprod[:, :].rearrange("p (n d) -> p n d", d=KS), AX.X, ALU.add).then_inc(band_ready, 1)
            for g in range(GROUPS):
                if g + 1 < GROUPS:
                    ysums(g + 1)
                for p in range(g * GROUP, (g + 1) * GROUP):
                    dve.wait_ge(yt_ready, p + 1)
                    nc.vector.tensor_reduce(maps[:, :, 1, 2 * p:2 * p + 2],
                                            bank[p % 2][:, 0:256].rearrange("p (t i c) -> p t i c", t=TILES, c=C),
                                            AX.X, ALU.max).then_inc(cmax_done, 1)
            dve.wait_ge(avg_ready, 1)
            nc.vector.tensor_copy(maps[:, :, 0, :].rearrange("p t (q i) -> p q t i", i=2),
                                  bank[3][:, 0:64].rearrange("p (q t i) -> p q t i", t=TILES, i=2)).then_inc(maps_ready, 1)
            dve.wait_ge(pb_ready, 1)
            dve.wait_ge(vec_in, 16)
            nc.vector.tensor_tensor(pbias[:, :], bank[5][:, 0:1], b_p, ALU.add).then_inc(pbias_ready, 1)

            def turn(k, slot, has, lap):
                p = k + 4
                x1 = at(xall, p) if has(4) else None

                def gn(i):
                    if i == 0:
                        wait(dve, x1_ready, p + 1)
                        op = nc.vector.bn_stats(bn6[:, :], x1)
                    else:
                        if i > 1:
                            wait(dve, gn_step, GN * p + i)
                        if i == 1:
                            op = nc.vector.bn_aggr(mv[:, :], bn6[:, :])
                        elif i == 2:
                            op = nc.vector.scalar_tensor_tensor(mv[:, 1:2], mv[:, 0:1], mv[:, 0:1], mv[:, 1:2], ALU.mult, ALU.add)
                        elif i == 3:
                            wait(dve, gs_ready, p + 1)
                            op = nc.vector.tensor_copy(gmv[:, :], gs_psum)
                        elif i == 4:
                            op = nc.vector.scalar_tensor_tensor(negvar[:, :], gmv[:, 0:1], gmv[:, 0:1], gmv[:, 1:2], ALU.mult, ALU.subtract)
                        else:
                            op = nc.vector.tensor_scalar(vareps[:, :], negvar[:, :], -1.0, EPS, ALU.mult, ALU.add)
                    op.then_inc(gn_step, 1)

                def gn_finish(i):
                    if i == 0:
                        wait(dve, rstd_ready, k + 4)
                        nc.vector.tensor_tensor(gna[:, :], rstd[:, :], w_gn, ALU.mult).then_inc(gn_step, 1)
                    elif i == 1:
                        wait(dve, gn_step, GN * (k + 3) + 7)
                        nc.vector.scalar_tensor_tensor(gnb[:, :], gmv[:, 0:1], gna[:, 0:1], b_gn, ALU.mult, ALU.subtract).then_inc(gn_step, 1)
                    else:
                        wait(dve, gn_step, GN * (k + 4))
                        wait(dve, v_ready, k + 1)
                        wait(dve, z_ready, k + 1)
                        nc.vector.tensor_scalar(xn[:, slot(3), :], at(xall, k + 3), gna[:, 0:1], gnb[:, 0:1], ALU.mult, ALU.subtract).then_inc(xn_ready, 1)

                def norm(i):
                    if i == 0:
                        wait(dve, pv_done, 2 * k)
                        op = nc.vector.transpose(otok[:, :, :].rearrange("p b c -> p (b c)"), o_bank[:, :])
                    else:
                        wait(dve, norm_step, 4 * (k - 1) + i)
                        if i == 1:
                            op = nc.vector.reciprocal(orec[:, :], otok[:, :, HD])
                        elif i == 2:
                            op = nc.vector.tensor_tensor(otok[:, :, 0:HD], otok[:, :, 0:HD],
                                                         orec[:, :].unsqueeze(2).broadcast_to([P, 2 * N // 32, HD]), ALU.mult)
                        else:
                            wait(dve, y_ready, k - 1)
                            op = nc.vector.transpose(onorm[:, :], otok[:, :, :].rearrange("p b c -> p (b c)"))
                    op.then_inc(norm_step, 1)

                def rowmax(u):
                    wait(dve, s_ready, UNITS * (k + 1) + u + 1)
                    if u == 0:
                        wait(dve, mt_ready, k - 1)
                    nc.vector.tensor_reduce(negmax[:, slot(1), u % HEADS, u // HEADS, :],
                                            s_bank[u % 2][:, :].rearrange("p (t n) -> p t n", t=TILES),
                                            AX.X, ALU.max, negate=True).then_inc(max_done, 1)

                for u in range(UNITS):
                    if has(4) and u == 5:
                        wait(dve, gn_step, GN * p + 1)
                    if has(1):
                        rowmax(u)
                    if has(-1) and u < 4:
                        norm(u)
                    if has(3) and u in (1, 2, 3):
                        gn_finish(u - 1)
                    if has(4) and u in (4, 5, 6):
                        gn(u - 4)
                if has(4):
                    for i in range(3, 6):
                        gn(i)
            pipeline(dve, turn)

        @block.tensor
        def _(pe):
            pe.wait_ge(con_in, 16)
            for g in range(GROUPS):
                pe.wait_ge(ytap_ready, g + 1)
                for d in range(KS):
                    mm = pe.matmul(bank[2][:, g * GROUP:(g + 1) * GROUP], con[:, C_BAND + d * P:C_BAND + (d + 1) * P],
                                   ytap[:, g, d, :], start=(d == 0), stop=(d == KS - 1))
                mm.then_inc(yconv_ready, 1)
                for p in range(g * GROUP, (g + 1) * GROUP):
                    pe.wait_ge(yc_ready, p + 1)
                    if p >= 2:
                        pe.wait_ge(cmax_done, p - 1)
                    for t in range(TILES):
                        mm = pe.transpose(bank[p % 2][:, t * P:(t + 1) * P], ycall[:, p, t * P:(t + 1) * P], ident)
                    mm.then_inc(yt_ready, 1)
                    for t in range(TILES):
                        c = 4 * p + 2 * t
                        mm = pe.matmul(bank[3][:, c:c + 2], ycall[:, p, t * P:(t + 1) * P], con[:, C_MEAN:C_MEAN + 2],
                                       start=True, stop=True)
            mm.then_inc(avg_ready, 1)
            pe.wait_ge(wall_in, 16)
            pe.wait_ge(vec_in, 16)
            for a in range(2):
                mm = pe.matmul(bank[5][64 * a:64 * a + 64, 0:1], w_p, b_v, start=True, stop=True)
            mm.then_inc(pb_ready, 1)
            pe.wait_ge(maps_ready, 1)
            pe.wait_ge(cmax_done, PAIRS)
            pe.wait_ge(toep_in, 16 * SIDE)
            for t in range(TILES):
                for m in range(2):
                    mm = pe.matmul(bank[4][0:IMAGES, 0:N], maps[:, t, m, :], toep[:, m, t, 2 * SIDE:2 * SIDE + N],
                                   start=(t == 0 and m == 0), stop=(t == TILES - 1 and m == 1))
            mm.then_inc(sconv_ready, 1)
            pe.wait_ge(identb_ready, 1)
            pe.wait_ge(fixed_ready, 2)
            pe.wait_ge(gate_ready, 1)
            pe.wait_ge(pbias_ready, 1)

            def turn(k, slot, has, lap):
                last = k + 3 if not isinstance(k, int) else min(k + 3, PAIRS - 1)
                gn_copied = GN * last + 4

                def st(u):
                    a, h = u // HEADS, u % HEADS
                    wait(pe, exp_done, UNITS * k + u - 1)
                    if u == 0:
                        wait(pe, mrow_in, 16 * (k + 1))
                    for t in range(TILES):
                        mm = pe.matmul(st_bank[u % 2][:, t * N:(t + 1) * N], ks[0:KQ + 1, slot(0), h, a, t * P:(t + 1) * P],
                                       qs[0:KQ + 1, slot(0), h, a, :], start=True, stop=True)
                    mm.then_inc(st_ready, 1)

                def s(u):
                    a, h = u // HEADS, u % HEADS
                    wait(pe, max_done, UNITS * (k + 1) + u - 1)
                    if u == 0:
                        wait(pe, stack_in[slot(1)], lap(1) * 96)
                    for t in range(TILES):
                        mm = pe.matmul(s_bank[u % 2][:, t * N:(t + 1) * N], qs[0:KQ, slot(1), h, a, t * P:(t + 1) * P],
                                       ks[0:KQ, slot(1), h, a, :], start=True, stop=True)
                    mm.then_inc(s_ready, 1)

                def pv(a):
                    wait(pe, exp_done, UNITS * k + HEADS * (a + 1))
                    if a == 0:
                        wait(pe, norm_step, 4 * (k - 1) + 1)
                        wait(pe, vs_ready, k + 1)
                    for t in range(TILES):
                        for h in range(HEADS):
                            mm = pe.matmul(o_bank[32 * h:32 * h + 32, a * N:(a + 1) * N], vs[:, slot(0), t, a, h, :],
                                           pt[:, HEADS * a + h, t, :], start=(t == 0), stop=(t == TILES - 1))
                    mm.then_inc(pv_done, 1)

                def qk():
                    wait(pe, xn_ready, k + 4)
                    wait(pe, z32_ready, k + 3)
                    for a in range(2):
                        mm = pe.matmul(z_bank[:, a * N:(a + 1) * N], w_qk[a], xn[:, slot(3), :], start=True, stop=True)
                    mm.then_inc(z_ready, 1)

                def v():
                    wait(pe, mrow_ready, k + 1)
                    wait(pe, xn_ready, k + 2)
                    for t in range(TILES):
                        mm = pe.matmul(v_psum[:, t * P:(t + 1) * P], xn[:, slot(1), t * P:(t + 1) * P], w_v, start=True, stop=True)
                    mm.then_inc(v_ready, 1)

                def proj():
                    wait(pe, norm_step, 4 * k)
                    wait(pe, gn_step, gn_copied)
                    for a in range(2):
                        mm = pe.matmul(y_psum[64 * a:64 * a + 64, :], w_p, onorm[:, a * N:(a + 1) * N], start=True, stop=True)
                    mm.then_inc(y_ready, 1)

                def groupstats():
                    wait(pe, gn_step, GN * (k + 4) + 3)
                    wait(pe, yo_ready, k)
                    mm = pe.matmul(gs_psum, groupavg, mv[:, :], start=True, stop=True)
                    mm.then_inc(gs_ready, 1)

                def maxt():
                    wait(pe, max_done, UNITS * (k + 2))
                    wait(pe, vs_ready, k + 2)
                    mm = pe.transpose(mt_psum, negmax[:, slot(1), :, :, :].rearrange("p h a t -> p (h a t)"), identb[:, :])
                    mm.then_inc(mt_ready, 1)

                for u in range(UNITS):
                    if has(0):
                        st(u)
                    if has(1):
                        s(u)
                    if u == 3 and has(3):
                        qk()
                    if u == 2 and has(1):
                        v()
                    if u == 5 and has(-1):
                        proj()
                    if u == 4 and has(0):
                        pv(0)
                if has(1):
                    maxt()
                if has(4):
                    groupstats()
                if has(0):
                    pv(1)
            pipeline(pe, turn)


def constants():
    import numpy as np
    c = np.zeros((P, C_END), np.float32)
    i, j = np.arange(P)[:, None], np.arange(P)[None, :]
    c[:, C_IDENT:C_IDENT + P] = i == j
    for d in range(KS):
        c[:, C_BAND + d * P:C_BAND + (d + 1) * P] = (i // C == j // C) & (i - j + KS // 2 == d)
    xp, d = np.arange(SIDE)[:, None], np.arange(KS)[None, :]
    for r in range(P):
        c[r, C_DX:C_DX + SIDE * KS] = (r % SIDE - xp + KS // 2 == d).reshape(-1)
    c[:, C_GROUP:C_GROUP + P] = 0.5 * (i // 2 == j // 2)
    c[:, C_MEAN:C_MEAN + 2] = (i // C == np.arange(2)[None, :]) / C
    return c


def kernel(x, L0_conv_w_c, L0_conv_w_s, L1_conv_gn_w, L1_conv_gn_b, L1_conv_qkv_w, L1_conv_qkv_b, L1_conv_proj_w, L1_conv_proj_b):
    import numpy as np
    import concourse.bacc as bacc
    from concourse.bass_utils import run_bass_kernel_spmd

    x, w_c, w_s, gn_w, gn_b, qkv_w, qkv_b, proj_w, proj_b = (np.asarray(a) for a in (
        x, L0_conv_w_c, L0_conv_w_s, L1_conv_gn_w, L1_conv_gn_b, L1_conv_qkv_w, L1_conv_qkv_b, L1_conv_proj_w, L1_conv_proj_b))
    w_rows = np.concatenate([w_c.reshape(-1), w_s[0, :, ::-1, :].reshape(-1)])
    qk = qkv_w[:2 * C].reshape(2, HEADS, HD, C).transpose(3, 0, 2, 1).reshape(C, 2 * C)
    w_all = np.zeros((P, 448), np.float32)
    w_all[0:C, 0:128] = qk
    w_all[C:P, 128:256] = qk
    w_all[0:C, 256:320] = qkv_w[2 * C:].T
    w_all[C:P, 320:384] = qkv_w[2 * C:].T
    vecs = np.zeros((P, 5), np.float32)
    vecs[:, 0] = qkv_b[:2 * C].reshape(2, HEADS, HD).transpose(0, 2, 1).reshape(-1)
    for h in range(HEADS):
        w_all[32 * h:32 * h + HD, 384:448] = proj_w[:, h * HD:(h + 1) * HD].T
        vecs[32 * h:32 * h + HD, 1] = qkv_b[2 * C + h * HD:2 * C + (h + 1) * HD]
    for i, v in ((2, proj_b), (3, gn_w), (4, gn_b)):
        vecs[0:C, i] = v
        vecs[C:P, i] = v
    arrays = {"x": x.reshape(IMAGES, C, N), "w_rows": w_rows, "vecs": vecs, "w_all": w_all, "consts": constants()}

    nc = bacc.Bacc("TRN2", target_bir_lowering=False, num_devices=1)
    args = [nc.dram_tensor(n, list(a.shape), F32, kind="ExternalInput").ap() for n, a in arrays.items()]
    out = nc.dram_tensor("out", [IMAGES, C, N], F32, kind="ExternalOutput").ap()
    program(nc, *args, out)
    r = run_bass_kernel_spmd(nc, [{n: np.ascontiguousarray(a) for n, a in arrays.items()}], core_ids=[0])
    return r.results[0]["out"].reshape(IMAGES, C, SIDE, SIDE)
```

```python
from contextlib import ExitStack

import concourse.bass as bass
from concourse import mybir

F32 = mybir.dt.float32
BF16 = mybir.dt.bfloat16
ALU = mybir.AluOpType
ACT = mybir.ActivationFunctionType
AX = mybir.AxisListType

P = 128
IMAGES, C, SIDE = 32, 64, 16
N = SIDE * SIDE
PAIRS = IMAGES // 2
HEADS, HD = 4, 16
TILES = N // P
KS = 5
GROUP = 4
GROUPS = PAIRS // GROUP
SLOTS = 6
KQ = SLOTS * HD
UNITS = 2 * HEADS
RING = 3
EPS = 1e-5
GN = 8
SCALE = float(HD) ** -0.5
KPAD = SIDE * (SIDE + KS - 1)

C_IDENT, C_BAND, C_DX, C_GROUP, C_MEAN = 0, 128, 768, 848, 976
C_END = 978


def program(nc, x, w_rows, vecs, w_all, consts, out):
    ctx = ExitStack()
    with ctx:
        def sb(name, shape, dt=F32):
            return ctx.enter_context(nc.sbuf_tensor(name, shape, dt))

        def sem(name):
            return ctx.enter_context(nc.semaphore(name))

        bank = [ctx.enter_context(nc.psum_tensor(f"bank{i}", [P, 512], F32)) for i in range(8)]
        parts_dram = nc.dram_tensor("parts_dram", [RING, 3, 2, HD, HEADS * 2 * N], BF16).ap()
        gate_dram = nc.dram_tensor("gate_dram", [IMAGES, N], F32).ap()

        xall = sb("xall", [P, PAIRS, N])
        ycall = sb("ycall", [P, PAIRS, N])
        gate = sb("gate", [P, PAIRS, N])
        con = sb("con", [P, C_END])
        wall = sb("wall", [P, 448])
        vec = sb("vec", [P, 5])
        wrow = sb("wrow", [P, KS + 2 * KS * KS])
        ident = con[:, C_IDENT:C_IDENT + P]
        groupavg = con[:, C_GROUP:C_GROUP + P]
        identb = sb("identb", [P, P], BF16)
        ysum = sb("ysum", [P, PAIRS])
        ytap = sb("ytap", [P, GROUPS, KS, GROUP])
        yscale = sb("yscale", [P, PAIRS])
        bandprod = sb("bandprod", [P, 2 * KS * SIDE * KS])
        bandrow = sb("bandrow", [P, 2, KS * SIDE])
        toep = sb("toep", [P, 2, TILES, KPAD])
        maps = sb("maps", [P, TILES, 2, IMAGES])
        gate_s = sb("gate_s", [IMAGES, N])
        pbias = sb("pbias", [P, 1])
        bn6 = sb("bn6", [P, 6])
        mv = sb("mv", [P, 2])
        gmv = sb("gmv", [P, 2])
        negvar = sb("negvar", [P, 1])
        vareps = sb("vareps", [P, 1])
        gna = sb("gna", [P, 1])
        gnb = sb("gnb", [P, 1])
        xn = sb("xn", [P, RING, N])
        z32 = sb("z32", [P, 2 * N])
        rest = sb("rest", [P, 2 * N])
        parts = sb("parts", [P, RING, 3, 2 * N], BF16)
        qs = sb("qs", [P, RING, HEADS, 2, N], BF16)
        ks = sb("ks", [P, RING, HEADS, 2, N], BF16)
        negmax = sb("negmax", [P, RING, HEADS, 2, TILES], BF16)
        maxrow = sb("maxrow", [16, RING, P], BF16)
        pt = sb("pt", [P, UNITS, TILES, N])
        vs = sb("vs", [P, RING, TILES, 2, HEADS, 2 * HD])
        rstd = sb("rstd", [P, 1])
        mhalf = sb("mhalf", [P, 1])
        o_tok = sb("otok", [P, 2 * N // 32, 32])
        orec = sb("orec", [P, 2 * N // 32])
        onorm = sb("onorm", [P, 2 * N])
        yo = sb("yo", [P, RING, N])

        b_qk, b_v, b_p, w_gn, b_gn = (vec[:, i:i + 1] for i in range(5))
        w_qk = [wall[:, a * P:(a + 1) * P] for a in range(2)]
        w_v = wall[:, 256:384]
        w_p = wall[:, 384:448]

        s_bank = [bank[0], bank[1]]
        st_bank = [bank[2], bank[3]]
        o_bank = bank[4]
        z_bank = bank[5]
        v_psum = bank[6][:, 0:256]
        mt_psum = bank[6][0:16, 320:384].bitcast(BF16)
        y_psum = bank[7][:, 0:256]
        gs_psum = bank[7][:, 0:2]

        rows_in, con_in, wall_in, vec_in = sem("rows_in"), sem("con_in"), sem("wall_in"), sem("vec_in")
        x_in = [sem(f"x_in{g}") for g in range(GROUPS)]
        mhalf_ready = sem("mhalf_ready")
        identb_ready, fixed_ready = sem("identb_ready"), sem("fixed_ready")
        ysum_ready, ytap_ready, yconv_ready, ys_ready = sem("ysum_ready"), sem("ytap_ready"), sem("yconv_ready"), sem("ys_ready")
        yc_ready, yt_ready, cmax_done, avg_ready, maps_ready = sem("yc_ready"), sem("yt_ready"), sem("cmax_done"), sem("avg_ready"), sem("maps_ready")
        prod_ready, band_ready, toep_zero, toep_in = sem("prod_ready"), sem("band_ready"), sem("toep_zero"), sem("toep_in")
        sconv_ready, gate_ready, gate_out = sem("sconv_ready"), sem("gate_ready"), sem("gate_out")
        gate_in = [sem(f"gate_in{g}") for g in range(GROUPS)]
        pb_ready, pbias_ready = sem("pb_ready"), sem("pbias_ready")

        u_ready, x1_ready = sem("u_ready"), sem("x1_ready")
        gn_step = sem("gn_step")
        gs_ready, xn_ready = sem("gs_ready"), sem("xn_ready")
        z_ready, v_ready = sem("z_ready"), sem("v_ready")
        p1_ready, z32_ready = sem("p1_ready"), sem("z32_ready")
        split_step = sem("split_step")
        parts_out, stack_in = sem("parts_out"), [sem(f"stack_in{r}") for r in range(RING)]
        s_ready, max_done = sem("s_ready"), sem("max_done")
        mt_ready, mrow_ready, mrow_in = sem("mt_ready"), sem("mrow_ready"), sem("mrow_in")
        st_ready, exp_done = sem("st_ready"), sem("exp_done")
        vs_ready, pv_done = sem("vs_ready"), sem("pv_done")
        norm_step, y_ready = sem("norm_step"), sem("y_ready")
        rstd_ready = sem("rstd_ready")
        yo_ready, out_ready = sem("yo_ready"), sem("out_ready")
        stored = sem("stored")

        def wait(eng, semaphore, value):
            if not isinstance(value, int) or value > 0:
                eng.wait_ge(semaphore, value)

        def at(t, p):
            return t[:, p, :] if isinstance(p, int) else t[:, bass.ds(p, 1), :].rearrange("p a n -> p (a n)")

        AHEAD, BEHIND = 5, 2
        LOOP_FROM, LOOP_TO = 2, 11

        def pipeline(eng, turn):
            def peeled(turns):
                for k in turns:
                    turn(k, lambda d, k=k: (k + d) % RING, lambda d, k=k: 0 <= k + d < PAIRS,
                         lambda d, k=k: (k + d) // RING + 1)
            peeled(range(-AHEAD, LOOP_FROM))
            with eng.Fori(0, (LOOP_TO - LOOP_FROM) // RING, 1) as laps:
                for j in range(LOOP_FROM, LOOP_FROM + RING):
                    turn(laps * RING + j, lambda d, j=j: (j + d) % RING, lambda d: True,
                         lambda d, j=j: laps + ((j + d) // RING + 1))
            peeled(range(LOOP_TO, PAIRS + BEHIND))

        block = ctx.enter_context(nc.Block())

        @block.sync
        def _(sp):
            sp.dma_start(xall[:, 0:GROUP, :], x[0:2 * GROUP].rearrange("(g i) c n -> (i c) g n", i=2)).then_inc(x_in[0], 16)
            sp.dma_start(wrow[:, :], w_rows.partition_broadcast(P)).then_inc(rows_in, 16)
            sp.dma_start(con[:, :], consts).then_inc(con_in, 16)
            for g in range(1, GROUPS):
                sp.dma_start(xall[:, g * GROUP:(g + 1) * GROUP, :],
                             x[2 * g * GROUP:2 * (g + 1) * GROUP].rearrange("(g i) c n -> (i c) g n", i=2)).then_inc(x_in[g], 16)
            sp.wait_ge(toep_zero, 1)
            sp.wait_ge(band_ready, 1)
            for t in range(TILES):
                for y in range(SIDE // TILES):
                    r = slice(SIDE * y, SIDE * (y + 1))
                    col = (SIDE // TILES * t + y) * SIDE
                    sp.dma_start(toep[r, :, t, col:col + KS * SIDE], bandrow[r, :, :]).then_inc(toep_in, 16)
            sp.dma_start(wall[:, :], w_all).then_inc(wall_in, 16)
            sp.dma_start(vec[:, :], vecs).then_inc(vec_in, 16)
            sp.wait_ge(gate_ready, 1)
            sp.dma_start(gate_dram, gate_s[:, :]).then_inc(gate_out, 16)
            sp.wait_ge(gate_out, 16)
            for g in range(GROUPS):
                for a in range(2):
                    src = gate_dram[2 * g * GROUP:2 * (g + 1) * GROUP, :].rearrange("(q i) n -> i q n", i=2)[a]
                    sp.dma_start(gate[C * a:C * (a + 1), g * GROUP:(g + 1) * GROUP, :],
                                 src.unsqueeze(0).broadcast_to([C, GROUP, N])).then_inc(gate_in[g], 16)

            def turn(k, slot, has, lap):
                if has(2):
                    r = slot(2)
                    wait(sp, parts_out, 16 * (k + 3))
                    for first, q_parts, k_parts in ((0, (0, 1, 2), (0, 0, 0)), (3, (0, 1), (1, 1)), (5, (0,), (2,))):
                        m = len(q_parts)
                        rows = slice(first * HD, (first + m) * HD)
                        src_q = parts_dram[r, 0:m, 0, :, :].rearrange("s d n -> d s n")
                        src_k = parts_dram[r, k_parts[0], 1, :, :].unsqueeze(1).broadcast_to([HD, m, HEADS * 2 * N])
                        sp.dma_start(qs[rows, r, :, :, :].rearrange("p h a n -> p (h a n)"), src_q).then_inc(stack_in[r], 16)
                        sp.dma_start(ks[rows, r, :, :, :].rearrange("p h a n -> p (h a n)"), src_k).then_inc(stack_in[r], 16)
                if has(-2):
                    wait(sp, out_ready, k - 1)
                    if isinstance(k, int):
                        dst = out[2 * (k - 2):2 * (k - 1)].rearrange("i c n -> (i c) n")
                    else:
                        dst = out[bass.ds(2 * (k - 2), 2)].rearrange("i c n -> (i c) n")
                    sp.dma_start(dst, at(xall, k - 2)).then_inc(stored, 16)
                if has(1):
                    wait(sp, mrow_ready, k + 2)
                    sp.dma_start(qs[KQ:KQ + 1, slot(1), :, :, :].rearrange("p h a (t n) -> p (h a t) n", t=TILES),
                                 maxrow[:, slot(1), :]).then_inc(mrow_in, 16)
                if has(3):
                    r = slot(3)
                    wait(sp, split_step, 3 * (k + 4))
                    sp.dma_start(parts_dram[r].rearrange("s g d (h n) -> (g d h) s n", h=HEADS), parts[:, r, :, :]).then_inc(parts_out, 16)
            pipeline(sp, turn)
            sp.wait_ge(stored, 16 * PAIRS)

        @block.gpsimd
        def _(pool):
            nc.gpsimd.memset(toep[:, :, :, :], 0.0).then_inc(toep_zero, 1)
            nc.gpsimd.memset(mhalf[:, :], -0.5).then_inc(mhalf_ready, 1)
            pool.wait_ge(mhalf_ready, 1)
            nc.gpsimd.memset(vs[:, :, :, :, :, :].rearrange("p r t a h d -> p (r t a h) d")[:, :, HD:2 * HD], 1.0).then_inc(fixed_ready, 1)
            pool.wait_ge(fixed_ready, 1)
            nc.gpsimd.memset(ks[KQ:KQ + 1, :, :, :, :], 1.0).then_inc(fixed_ready, 1)

            pool.wait_ge(fixed_ready, 2)

            def turn(k, slot, has, lap):
                if has(5):
                    for g in [(k + 5) // GROUP] if isinstance(k, int) else range(1, GROUPS):
                        pool.wait_ge(gate_in[g], 32)
                    nc.gpsimd.tensor_tensor(at(ycall, k + 5), at(ycall, k + 5), at(gate, k + 5), ALU.mult).then_inc(u_ready, 1)
                    pool.wait_ge(u_ready, k + 6)
                    nc.gpsimd.tensor_tensor(at(xall, k + 5), at(ycall, k + 5), at(xall, k + 5), ALU.add).then_inc(x1_ready, 1)
                if has(4):
                    wait(pool, gn_step, GN * (k + 4) + 6)
                    nc.gpsimd.tensor_tensor(rstd[:, :], vareps[:, :], mhalf[:, :], ALU.pow).then_inc(rstd_ready, 1)
                r = slot(3)
                if has(3):
                    wait(pool, p1_ready, k + 4)
                    wait(pool, z32_ready, k + 4)
                    wait(pool, split_step, 3 * (k + 3))
                    nc.gpsimd.tensor_tensor(rest[:, :], z32[:, :], parts[:, r, 0, :], ALU.subtract).then_inc(split_step, 1)
                    wait(pool, split_step, 3 * (k + 3) + 1)
                if has(-2):
                    wait(pool, yo_ready, k - 1)
                    nc.gpsimd.tensor_tensor(at(xall, k - 2), yo[:, slot(-2), :], at(xall, k - 2), ALU.add).then_inc(out_ready, 1)
                if has(3):
                    nc.gpsimd.tensor_scalar(parts[:, r, 1, :], rest[:, :], 1.0, 0.0, ALU.mult, ALU.add).then_inc(split_step, 1)
                    wait(pool, split_step, 3 * (k + 3) + 2)
                    nc.gpsimd.tensor_tensor(parts[:, r, 2, :], rest[:, :], parts[:, r, 1, :], ALU.subtract).then_inc(split_step, 1)
            pipeline(pool, turn)

        @block.scalar
        def _(act):
            act.wait_ge(con_in, 16)
            nc.scalar.copy(identb[:, :], ident).then_inc(identb_ready, 1)
            for g in range(GROUPS):
                act.wait_ge(yconv_ready, g + 1)
                nc.scalar.activation(yscale[:, g * GROUP:(g + 1) * GROUP], bank[2][:, g * GROUP:(g + 1) * GROUP],
                                     ACT.Copy, scale=1.0 / N).then_inc(ys_ready, 1)
                act.wait_ge(ys_ready, g + 1)
                for p in range(g * GROUP, (g + 1) * GROUP):
                    nc.scalar.activation(ycall[:, p, :], xall[:, p, :], ACT.Sigmoid,
                                         scale=yscale[:, p:p + 1]).then_inc(yc_ready, 1)
            act.wait_ge(sconv_ready, 1)
            nc.scalar.activation(gate_s[:, :], bank[4][0:IMAGES, 0:N], ACT.Sigmoid).then_inc(gate_ready, 1)

            def turn(k, slot, has, lap):
                def exps(u0, u1):
                    for u in range(u0, u1):
                        wait(act, st_ready, UNITS * k + u + 1)
                        if u % HEADS == 0:
                            wait(act, pv_done, 2 * (k - 1) + u // HEADS + 1)
                        nc.scalar.activation(pt[:, u, :, :].rearrange("p t n -> p (t n)"), st_bank[u % 2][:, :], ACT.Exp,
                                             scale=SCALE).then_inc(exp_done, 1)
                if has(0):
                    exps(0, 2)
                if has(3):
                    wait(act, z_ready, k + 4)
                    wait(act, parts_out, 16 * (k + 1))
                    nc.scalar.activation(parts[:, slot(3), 0, :], z_bank[:, :], ACT.Identity, bias=b_qk).then_inc(p1_ready, 1)
                    wait(act, split_step, 3 * (k + 2) + 1)
                    nc.scalar.activation(z32[:, :], z_bank[:, :], ACT.Identity, bias=b_qk).then_inc(z32_ready, 1)
                if has(0):
                    exps(2, 5)
                if has(1):
                    wait(act, v_ready, k + 2)
                    nc.scalar.copy(vs[:, slot(1), :, :, :, :].rearrange("p t a h d -> p (t a h) d")[:, :, 0:HD],
                                   v_psum.rearrange("p (g d) -> p g d", d=HD)).then_inc(vs_ready, 1)
                if has(0):
                    exps(5, 8)
                if has(1):
                    wait(act, mt_ready, k + 2)
                    wait(act, mrow_in, 16 * (k - 1))
                    nc.scalar.copy(maxrow[:, slot(1), :], mt_psum).then_inc(mrow_ready, 1)
                if has(4):
                    wait(act, gn_step, GN * (k + 5))
                    wait(act, v_ready, k + 2)
                    nc.scalar.activation(xn[:, slot(4), :], at(xall, k + 4), ACT.Identity, bias=gnb[:, 0:1], scale=gna[:, 0:1]).then_inc(xn_ready, 1)
                if has(-1):
                    wait(act, y_ready, k)
                    nc.scalar.activation(yo[:, slot(-1), :], y_psum, ACT.Identity, bias=pbias[:, 0:1]).then_inc(yo_ready, 1)
            act.wait_ge(pbias_ready, 1)
            pipeline(act, turn)

        @block.vector
        def _(dve):
            def ysums(g):
                dve.wait_ge(x_in[g], 16)
                nc.vector.tensor_reduce(ysum[:, g * GROUP:(g + 1) * GROUP], xall[:, g * GROUP:(g + 1) * GROUP, :],
                                        AX.X, ALU.add).then_inc(ysum_ready, 1)
                dve.wait_ge(ysum_ready, g + 1)
                dve.wait_ge(rows_in, 16)
                taps = wrow[:, 0:KS].unsqueeze(2).broadcast_to([P, KS, GROUP])
                sums = ysum[:, g * GROUP:(g + 1) * GROUP].unsqueeze(1).broadcast_to([P, KS, GROUP])
                nc.vector.tensor_tensor(ytap[:, g, :, :], taps, sums, ALU.mult).then_inc(ytap_ready, 1)

            ysums(0)
            dve.wait_ge(con_in, 16)
            rows = 2 * KS
            dx_mask = con[:, C_DX:C_DX + SIDE * KS].rearrange("p (x d) -> p x d", d=KS).unsqueeze(1).broadcast_to([P, rows, SIDE, KS])
            dx_w = wrow[:, KS:KS + rows * KS].rearrange("p (r d) -> p r d", d=KS).unsqueeze(2).broadcast_to([P, rows, SIDE, KS])
            nc.vector.tensor_tensor(bandprod[:, :].rearrange("p (r x d) -> p r x d", r=rows, d=KS), dx_mask, dx_w,
                                    ALU.mult).then_inc(prod_ready, 1)
            dve.wait_ge(prod_ready, 1)
            nc.vector.tensor_reduce(bandrow[:, :, :].rearrange("p m n -> p (m n)"),
                                    bandprod[:, :].rearrange("p (n d) -> p n d", d=KS), AX.X, ALU.add).then_inc(band_ready, 1)
            for g in range(GROUPS):
                if g + 1 < GROUPS:
                    ysums(g + 1)
                for p in range(g * GROUP, (g + 1) * GROUP):
                    dve.wait_ge(yt_ready, p + 1)
                    nc.vector.tensor_reduce(maps[:, :, 1, 2 * p:2 * p + 2],
                                            bank[p % 2][:, 0:256].rearrange("p (t i c) -> p t i c", t=TILES, c=C),
                                            AX.X, ALU.max).then_inc(cmax_done, 1)
            dve.wait_ge(avg_ready, 1)
            nc.vector.tensor_copy(maps[:, :, 0, :].rearrange("p t (q i) -> p q t i", i=2),
                                  bank[3][:, 0:64].rearrange("p (q t i) -> p q t i", t=TILES, i=2)).then_inc(maps_ready, 1)
            dve.wait_ge(pb_ready, 1)
            dve.wait_ge(vec_in, 16)
            nc.vector.tensor_tensor(pbias[:, :], bank[5][:, 0:1], b_p, ALU.add).then_inc(pbias_ready, 1)

            def turn(k, slot, has, lap):
                p = k + 5
                x1 = at(xall, p) if has(5) else None

                def gn(i):
                    if i == 0:
                        wait(dve, x1_ready, p + 1)
                        op = nc.vector.bn_stats(bn6[:, :], x1)
                    else:
                        if i > 1:
                            wait(dve, gn_step, GN * p + i)
                        if i == 1:
                            op = nc.vector.bn_aggr(mv[:, :], bn6[:, :])
                        elif i == 2:
                            op = nc.vector.scalar_tensor_tensor(mv[:, 1:2], mv[:, 0:1], mv[:, 0:1], mv[:, 1:2], ALU.mult, ALU.add)
                        elif i == 3:
                            wait(dve, gs_ready, p + 1)
                            wait(dve, gn_step, GN * p)
                            op = nc.vector.tensor_scalar(gmv[:, :], gs_psum, -1.0, None, ALU.mult)
                        elif i == 4:
                            op = nc.vector.scalar_tensor_tensor(negvar[:, :], gmv[:, 0:1], gmv[:, 0:1], gmv[:, 1:2], ALU.mult, ALU.add)
                        else:
                            op = nc.vector.tensor_scalar(vareps[:, :], negvar[:, :], -1.0, EPS, ALU.mult, ALU.add)
                    op.then_inc(gn_step, 1)

                def gn_finish(i):
                    if i == 0:
                        wait(dve, rstd_ready, k + 5)
                        wait(dve, xn_ready, k + 4)
                        nc.vector.tensor_tensor(gna[:, :], rstd[:, :], w_gn, ALU.mult).then_inc(gn_step, 1)
                    else:
                        wait(dve, gn_step, GN * (k + 4) + 7)
                        nc.vector.scalar_tensor_tensor(gnb[:, :], gmv[:, 0:1], gna[:, 0:1], b_gn, ALU.mult, ALU.add).then_inc(gn_step, 1)

                def norm(i):
                    if i == 0:
                        wait(dve, pv_done, 2 * k)
                        op = nc.vector.transpose(o_tok[:, :, :].rearrange("p b c -> p (b c)"), o_bank[:, :])
                    else:
                        wait(dve, norm_step, 4 * (k - 1) + i)
                        if i == 1:
                            op = nc.vector.reciprocal(orec[:, :], o_tok[:, :, HD])
                        elif i == 2:
                            op = nc.vector.tensor_tensor(o_tok[:, :, 0:HD], o_tok[:, :, 0:HD],
                                                         orec[:, :].unsqueeze(2).broadcast_to([P, 2 * N // 32, HD]), ALU.mult)
                        else:
                            wait(dve, y_ready, k - 1)
                            op = nc.vector.transpose(onorm[:, :], o_tok[:, :, :].rearrange("p b c -> p (b c)"))
                    op.then_inc(norm_step, 1)

                def rowmax(u):
                    wait(dve, s_ready, UNITS * (k + 1) + u + 1)
                    if u == 0:
                        wait(dve, mt_ready, k - 1)
                    nc.vector.tensor_reduce(negmax[:, slot(1), u % HEADS, u // HEADS, :],
                                            s_bank[u % 2][:, :].rearrange("p (t n) -> p t n", t=TILES),
                                            AX.X, ALU.max, negate=True).then_inc(max_done, 1)

                for u in range(UNITS):
                    if has(1):
                        rowmax(u)
                    if has(-1) and u == 3:
                        norm(0)
                if has(4):
                    gn_finish(0)
                if has(-1):
                    norm(1)
                if has(4):
                    gn_finish(1)
                if has(5):
                    gn(0)
                    wait(dve, gn_step, GN * p + 1)
                if has(-1):
                    norm(2)
                if has(5):
                    gn(1)
                    gn(2)
                if has(-1):
                    norm(3)
                if has(5):
                    for i in range(3, 6):
                        gn(i)
            pipeline(dve, turn)

        @block.tensor
        def _(pe):
            pe.wait_ge(con_in, 16)
            for g in range(GROUPS):
                pe.wait_ge(ytap_ready, g + 1)
                for d in range(KS):
                    mm = pe.matmul(bank[2][:, g * GROUP:(g + 1) * GROUP], con[:, C_BAND + d * P:C_BAND + (d + 1) * P],
                                   ytap[:, g, d, :], start=(d == 0), stop=(d == KS - 1))
                mm.then_inc(yconv_ready, 1)
                for p in range(g * GROUP, (g + 1) * GROUP):
                    pe.wait_ge(yc_ready, p + 1)
                    if p >= 2:
                        pe.wait_ge(cmax_done, p - 1)
                    for t in range(TILES):
                        mm = pe.transpose(bank[p % 2][:, t * P:(t + 1) * P], ycall[:, p, t * P:(t + 1) * P], ident)
                    mm.then_inc(yt_ready, 1)
                    for t in range(TILES):
                        c = 4 * p + 2 * t
                        mm = pe.matmul(bank[3][:, c:c + 2], ycall[:, p, t * P:(t + 1) * P], con[:, C_MEAN:C_MEAN + 2],
                                       start=True, stop=True)
            mm.then_inc(avg_ready, 1)
            pe.wait_ge(wall_in, 16)
            pe.wait_ge(vec_in, 16)
            for a in range(2):
                mm = pe.matmul(bank[5][64 * a:64 * a + 64, 0:1], w_p, b_v, start=True, stop=True)
            mm.then_inc(pb_ready, 1)
            pe.wait_ge(maps_ready, 1)
            pe.wait_ge(cmax_done, PAIRS)
            pe.wait_ge(toep_in, 16 * SIDE)
            for t in range(TILES):
                for m in range(2):
                    mm = pe.matmul(bank[4][0:IMAGES, 0:N], maps[:, t, m, :], toep[:, m, t, 2 * SIDE:2 * SIDE + N],
                                   start=(t == 0 and m == 0), stop=(t == TILES - 1 and m == 1))
            mm.then_inc(sconv_ready, 1)
            pe.wait_ge(identb_ready, 1)
            pe.wait_ge(fixed_ready, 2)
            pe.wait_ge(gate_ready, 1)
            pe.wait_ge(pbias_ready, 1)

            def turn(k, slot, has, lap):
                def st(u):
                    a, h = u // HEADS, u % HEADS
                    wait(pe, exp_done, UNITS * k + u - 1)
                    if u == 0:
                        wait(pe, mrow_in, 16 * (k + 1))
                    for t in range(TILES):
                        mm = pe.matmul(st_bank[u % 2][:, t * N:(t + 1) * N], ks[0:KQ + 1, slot(0), h, a, t * P:(t + 1) * P],
                                       qs[0:KQ + 1, slot(0), h, a, :], start=True, stop=True)
                    mm.then_inc(st_ready, 1)

                def s(u):
                    a, h = u // HEADS, u % HEADS
                    wait(pe, max_done, UNITS * (k + 1) + u - 1)
                    if u == 0:
                        wait(pe, stack_in[slot(1)], lap(1) * 96)
                    for t in range(TILES):
                        mm = pe.matmul(s_bank[u % 2][:, t * N:(t + 1) * N], qs[0:KQ, slot(1), h, a, t * P:(t + 1) * P],
                                       ks[0:KQ, slot(1), h, a, :], start=True, stop=True)
                    mm.then_inc(s_ready, 1)

                def pv(d, a):
                    wait(pe, exp_done, UNITS * (k + d) + HEADS * (a + 1))
                    if a == 0:
                        wait(pe, norm_step, 4 * (k + d - 1) + 1)
                        wait(pe, vs_ready, k + d + 1)
                    for t in range(TILES):
                        for h in range(HEADS):
                            mm = pe.matmul(o_bank[32 * h:32 * h + 32, a * N:(a + 1) * N], vs[:, slot(d), t, a, h, :],
                                           pt[:, HEADS * a + h, t, :], start=(t == 0), stop=(t == TILES - 1))
                    mm.then_inc(pv_done, 1)

                def qk():
                    wait(pe, xn_ready, k + 4)
                    wait(pe, z32_ready, k + 3)
                    for a in range(2):
                        mm = pe.matmul(z_bank[:, a * N:(a + 1) * N], w_qk[a], xn[:, slot(3), :], start=True, stop=True)
                    mm.then_inc(z_ready, 1)

                def v():
                    wait(pe, mrow_ready, k + 1)
                    wait(pe, xn_ready, k + 2)
                    for t in range(TILES):
                        mm = pe.matmul(v_psum[:, t * P:(t + 1) * P], xn[:, slot(1), t * P:(t + 1) * P], w_v, start=True, stop=True)
                    mm.then_inc(v_ready, 1)

                def proj():
                    wait(pe, norm_step, 4 * k)
                    if has(5):
                        wait(pe, gn_step, GN * (k + 5) + 4)
                    else:
                        wait(pe, yo_ready, k - 1)
                    for a in range(2):
                        mm = pe.matmul(y_psum[64 * a:64 * a + 64, :], w_p, onorm[:, a * N:(a + 1) * N], start=True, stop=True)
                    mm.then_inc(y_ready, 1)

                def groupstats():
                    wait(pe, gn_step, GN * (k + 5) + 3)
                    wait(pe, yo_ready, k - 1)
                    mm = pe.matmul(gs_psum, groupavg, mv[:, :], start=True, stop=True)
                    mm.then_inc(gs_ready, 1)

                def maxt():
                    wait(pe, max_done, UNITS * (k + 2))
                    wait(pe, vs_ready, k + 2)
                    mm = pe.transpose(mt_psum, negmax[:, slot(1), :, :, :].rearrange("p h a t -> p (h a t)"), identb[:, :])
                    mm.then_inc(mt_ready, 1)

                if has(1):
                    s(0)
                    s(1)
                for u in range(UNITS):
                    if has(0):
                        st(u)
                    if has(-1) and u == 0:
                        pv(-1, 1)
                    if has(3) and u == 1:
                        qk()
                    if has(1) and u == 2:
                        v()
                    if has(0) and u == 6:
                        pv(0, 0)
                    if has(1) and u + 2 < UNITS:
                        s(u + 2)
                if has(1):
                    maxt()
                if has(5):
                    groupstats()
                if has(-1):
                    proj()
            pipeline(pe, turn)


def constants():
    import numpy as np
    c = np.zeros((P, C_END), np.float32)
    i, j = np.arange(P)[:, None], np.arange(P)[None, :]
    c[:, C_IDENT:C_IDENT + P] = i == j
    for d in range(KS):
        c[:, C_BAND + d * P:C_BAND + (d + 1) * P] = (i // C == j // C) & (i - j + KS // 2 == d)
    xp, d = np.arange(SIDE)[:, None], np.arange(KS)[None, :]
    for r in range(P):
        c[r, C_DX:C_DX + SIDE * KS] = (r % SIDE - xp + KS // 2 == d).reshape(-1)
    c[:, C_GROUP:C_GROUP + P] = 0.5 * (i // 2 == j // 2)
    c[:, C_MEAN:C_MEAN + 2] = (i // C == np.arange(2)[None, :]) / C
    return c


def kernel(x, L0_conv_w_c, L0_conv_w_s, L1_conv_gn_w, L1_conv_gn_b, L1_conv_qkv_w, L1_conv_qkv_b, L1_conv_proj_w, L1_conv_proj_b):
    import numpy as np
    import concourse.bacc as bacc
    from concourse.bass_utils import run_bass_kernel_spmd

    x, w_c, w_s, gn_w, gn_b, qkv_w, qkv_b, proj_w, proj_b = (np.asarray(a) for a in (
        x, L0_conv_w_c, L0_conv_w_s, L1_conv_gn_w, L1_conv_gn_b, L1_conv_qkv_w, L1_conv_qkv_b, L1_conv_proj_w, L1_conv_proj_b))
    w_rows = np.concatenate([w_c.reshape(-1), w_s[0, :, ::-1, :].reshape(-1)])
    qk = qkv_w[:2 * C].reshape(2, HEADS, HD, C).transpose(3, 0, 2, 1).reshape(C, 2 * C)
    w_all = np.zeros((P, 448), np.float32)
    w_all[0:C, 0:128] = qk
    w_all[C:P, 128:256] = qk
    w_all[0:C, 256:320] = qkv_w[2 * C:].T
    w_all[C:P, 320:384] = qkv_w[2 * C:].T
    vecs = np.zeros((P, 5), np.float32)
    vecs[:, 0] = qkv_b[:2 * C].reshape(2, HEADS, HD).transpose(0, 2, 1).reshape(-1)
    for h in range(HEADS):
        w_all[32 * h:32 * h + HD, 384:448] = proj_w[:, h * HD:(h + 1) * HD].T
        vecs[32 * h:32 * h + HD, 1] = qkv_b[2 * C + h * HD:2 * C + (h + 1) * HD]
    for i, v in ((2, proj_b), (3, gn_w), (4, gn_b)):
        vecs[0:C, i] = v
        vecs[C:P, i] = v
    arrays = {"x": x.reshape(IMAGES, C, N), "w_rows": w_rows, "vecs": vecs, "w_all": w_all, "consts": constants()}

    nc = bacc.Bacc("TRN2", target_bir_lowering=False, num_devices=1)
    args = [nc.dram_tensor(n, list(a.shape), F32, kind="ExternalInput").ap() for n, a in arrays.items()]
    out = nc.dram_tensor("out", [IMAGES, C, N], F32, kind="ExternalOutput").ap()
    program(nc, *args, out)
    r = run_bass_kernel_spmd(nc, [{n: np.ascontiguousarray(a) for n, a in arrays.items()}], core_ids=[0])
    return r.results[0]["out"].reshape(IMAGES, C, SIDE, SIDE)
```

```python
from contextlib import ExitStack

import concourse.bass as bass
from concourse import mybir

F32 = mybir.dt.float32
BF16 = mybir.dt.bfloat16
ALU = mybir.AluOpType
ACT = mybir.ActivationFunctionType
AX = mybir.AxisListType

P = 128
IMAGES, C, SIDE = 32, 64, 16
N = SIDE * SIDE
PAIRS = IMAGES // 2
HEADS, HD = 4, 16
TILES = N // P
KS = 5
GROUP = 4
GROUPS = PAIRS // GROUP
SLOTS = 6
KQ = SLOTS * HD
UNITS = 2 * HEADS
RING = 4
EARLY = (0, 1, GROUP)
EPS = 1e-5
LEAD = HEADS
SCALE = float(HD) ** -0.5
KPAD = SIDE * (SIDE + KS - 1)

C_DX, C_BAND = 0, KS * SIDE
PADC = C + KS - 1
C_IDENT = C_BAND + 2 * PADC
C_MEAN = C_IDENT + P
C_GROUP = C_MEAN + 2
C_END = C_GROUP + P
TSTRIDE = KPAD + P


def program(nc, x, w_rows, vecs, w_all, select, consts, out):
    ctx = ExitStack()
    with ctx:
        def sb(name, shape, dt=F32):
            return ctx.enter_context(nc.sbuf_tensor(name, shape, dt))

        def sem(name):
            return ctx.enter_context(nc.semaphore(name))

        bank = [ctx.enter_context(nc.psum_tensor(f"bank{i}", [P, 512], F32)) for i in range(8)]
        parts_dram = nc.dram_tensor("parts_dram", [RING, 3, 2, HD, HEADS * 2 * N], BF16).ap()
        gate_dram = nc.dram_tensor("gate_dram", [IMAGES, N], F32).ap()

        xall = sb("xall", [P, PAIRS, N])
        ycall = sb("ycall", [P, PAIRS, N])
        gate = sb("gate", [P, PAIRS, N])
        con = sb("con", [P, C_END])
        wall = sb("wall", [P, 448])
        vec = sb("vec", [P, 5])
        wrow = sb("wrow", [P, KS + 2 * KS * KS])
        ident = con[:, C_IDENT:C_IDENT + P]
        groupavg = con[:, C_GROUP:C_GROUP + P]
        identb = sb("identb", [P, P], BF16)
        ysum = sb("ysum", [P, PAIRS])
        tapprod = sb("tapprod", [P, KS, P])
        band = sb("band", [P, P])
        yscale = sb("yscale", [P, PAIRS])
        bandprod = sb("bandprod", [P, 2 * KS * SIDE * KS])
        bandrow = sb("bandrow", [P, TILES, 2, KS * SIDE])
        toep = sb("toep", [P, 2 * TILES * TSTRIDE])
        junk = sb("junk", [P, 1])
        maps = sb("maps", [P, TILES, 2, IMAGES])
        gate_s = sb("gate_s", [IMAGES, 2, N])
        sel = sb("sel", [2 * GROUP, 2 * P])
        warm = sb("warm", [P, 512], BF16)
        pbias = sb("pbias", [P, 1])
        bn6 = sb("bn6", [P, 6])
        mv = sb("mv", [P, 2])
        gmv = sb("gmv", [P, 2])
        sq = sb("sq", [P, 1])
        negvar = sb("negvar", [P, 1])
        vareps = sb("vareps", [P, 1])
        gna = sb("gna", [P, 1])
        gnb = sb("gnb", [P, 1])
        xn = sb("xn", [P, RING, N])
        z32 = sb("z32", [P, 2 * N])
        rest = sb("rest", [P, 2 * N])
        parts = sb("parts", [P, RING, 3, 2 * N], BF16)
        qs = sb("qs", [P, RING, HEADS, 2, N], BF16)
        ks = sb("ks", [P, RING, HEADS, 2, N], BF16)
        negmax = sb("negmax", [P, RING, HEADS, 2, TILES], BF16)
        maxrow = sb("maxrow", [16, RING, P], BF16)
        pt = sb("pt", [P, UNITS, TILES, N])
        vs = sb("vs", [P, RING, TILES, 2, HEADS, 2 * HD])
        rstd = sb("rstd", [P, 1])
        mhalf = sb("mhalf", [P, 1])
        eps = sb("eps", [P, 1])
        o_tok = sb("otok", [P, 2 * N // 32, 32])
        orec = sb("orec", [P, 2 * N // 32])
        onorm = sb("onorm", [P, 2 * N])
        yo = sb("yo", [P, RING, N])

        b_qk, b_v, b_p, w_gn, b_gn = (vec[:, i:i + 1] for i in range(5))
        w_qk = [wall[:, a * P:(a + 1) * P] for a in range(2)]
        w_v = wall[:, 256:384]
        w_p = wall[:, 384:448]

        yconv_bank, gate_bank = [bank[2], bank[6]], {0: bank[3], 1: bank[4], GROUP: bank[2]}
        s_bank = [bank[0], bank[1]]
        st_bank = [bank[2], bank[3]]
        o_bank = bank[4]
        z_bank = bank[5]
        v_psum = bank[6][:, 0:256]
        mt_psum = bank[6][0:16, 320:384].bitcast(BF16)
        y_psum = bank[7][:, 0:256]
        gs_psum = bank[7][:, 0:2]

        rows_in, con_in, ident_in = sem("rows_in"), sem("con_in"), sem("ident_in")
        wall_in, vec_in, sel_in = sem("wall_in"), sem("vec_in"), sem("sel_in")
        x_in = [sem(f"x_in{g}") for g in range(GROUPS)]
        mhalf_ready, eps_ready = sem("mhalf_ready"), sem("eps_ready")
        identb_ready, fixed_ready = sem("identb_ready"), sem("fixed_ready")
        ysum_ready, yconv_ready, ys_ready = sem("ysum_ready"), sem("yconv_ready"), sem("ys_ready")
        yc_ready, yt_ready, maps_done = sem("yc_ready"), sem("yt_ready"), sem("maps_done")
        warm_ready, spread_ready = sem("warm_ready"), sem("spread_ready")
        prod_ready, band_ready, toep_zero, toep_in = sem("prod_ready"), sem("band_ready"), sem("toep_zero"), sem("toep_in")
        tapprod_ready, tap_ready, tables_ready = sem("tapprod_ready"), sem("tap_ready"), sem("tables_ready")
        sconv_ready, gate_ready = sem("sconv_ready"), sem("gate_ready")
        gate_out = [sem("gate_out0"), sem("gate_out1")]
        gate_in = [sem(f"gate_in{g}") for g in range(GROUPS)]
        pb_ready, pbias_ready = sem("pb_ready"), sem("pbias_ready")

        u_ready, x1_ready = sem("u_ready"), sem("x1_ready")
        gn_stat, gn_mean, gn_shift = sem("gn_stat"), sem("gn_mean"), sem("gn_shift")
        gs_ready, xn_ready = sem("gs_ready"), sem("xn_ready")
        z_ready, v_ready = sem("z_ready"), sem("v_ready")
        p1_ready, z32_ready = sem("p1_ready"), sem("z32_ready")
        split_step = sem("split_step")
        parts_out = sem("parts_out")
        stack_in = [sem(f"stack_in{r}") for r in range(RING)]
        s_ready, max_done = sem("s_ready"), sem("max_done")
        mt_ready, mrow_ready, mrow_in = sem("mt_ready"), sem("mrow_ready"), sem("mrow_in")
        st_ready, exp_done = sem("st_ready"), sem("exp_done")
        vs_ready, pv_done = sem("vs_ready"), sem("pv_done")
        norm_step, y_ready = sem("norm_step"), sem("y_ready")
        sq_ready, negvar_ready, vareps_ready = sem("sq_ready"), sem("negvar_ready"), sem("vareps_ready")
        rstd_ready, gn_scale = sem("rstd_ready"), sem("gn_scale")
        yo_ready, out_ready = sem("yo_ready"), sem("out_ready")
        stored = sem("stored")

        def wait(eng, semaphore, value):
            if not isinstance(value, int) or value > 0:
                eng.wait_ge(semaphore, value)

        def at(t, p):
            return t[:, p, :] if isinstance(p, int) else t[:, bass.ds(p, 1), :].rearrange("p a n -> p (a n)")

        AHEAD, BEHIND = 5, 2
        LOOP_FROM, LOOP_TO = 2, 10

        def stands_in(aside, k, u):
            if isinstance(k, int) and (k, u) in aside:
                aside[k, u]()

        def pipeline(eng, turn):
            def peeled(turns):
                for k in turns:
                    turn(k, lambda d, k=k: (k + d) % RING, lambda d, k=k: 0 <= k + d < PAIRS,
                         lambda d, k=k: (k + d) // RING + 1)
            peeled(range(-AHEAD, LOOP_FROM))
            with eng.Fori(0, (LOOP_TO - LOOP_FROM) // RING, 1) as laps:
                for j in range(LOOP_FROM, LOOP_FROM + RING):
                    turn(laps * RING + j, lambda d, j=j: (j + d) % RING, lambda d: True,
                         lambda d, j=j: laps + ((j + d) // RING + 1))
            peeled(range(LOOP_TO, PAIRS + BEHIND))

        def gate_write(eng, chunk, first, last):
            eng.wait_ge(gate_ready, chunk + 1)
            eng.dma_start(gate_dram[first:last, :], gate_s[0:last - first, chunk, :]).then_inc(gate_out[chunk], 16)

        def gate_read(eng, g):
            eng.wait_ge(gate_out[min(g, 1)], 16)
            for a in range(2):
                src = gate_dram[2 * g * GROUP:2 * (g + 1) * GROUP, :].rearrange("(q i) n -> i q n", i=2)[a]
                eng.dma_start(gate[C * a:C * (a + 1), g * GROUP:(g + 1) * GROUP, :],
                              src.unsqueeze(0).broadcast_to([C, GROUP, N])).then_inc(gate_in[g], 16)

        block = ctx.enter_context(nc.Block())

        @block.sync
        def _(sp):
            sp.dma_start(wrow[:, :], w_rows.partition_broadcast(P)).then_inc(rows_in, 16)
            sp.dma_start(con[:, 0:C_IDENT], consts[:, 0:C_IDENT]).then_inc(con_in, 16)
            for g in range(GROUPS):
                sp.dma_start(xall[:, g * GROUP:(g + 1) * GROUP, :],
                             x[2 * g * GROUP:2 * (g + 1) * GROUP].rearrange("(g i) c n -> (i c) g n", i=2)).then_inc(x_in[g], 16)
                if g == 0:
                    sp.dma_start(sel[:, :], select).then_inc(sel_in, 16)
                    sp.dma_start(con[:, C_IDENT:C_END], consts[:, C_IDENT:C_END]).then_inc(ident_in, 16)
            sp.wait_ge(toep_zero, 1)
            sp.wait_ge(band_ready, 2)
            for y in range(SIDE // TILES):
                r = slice(SIDE * y, SIDE * (y + 1))
                dst = toep[r, :].rearrange("p (a c) -> p a c", c=TSTRIDE)[:, :, y * SIDE:(y + KS) * SIDE]
                sp.dma_start(dst, bandrow[r, :, :, :].rearrange("p t m n -> p (t m) n")).then_inc(toep_in, 16)
            sp.dma_start(wall[:, :], w_all).then_inc(wall_in, 16)
            sp.dma_start(vec[:, :], vecs).then_inc(vec_in, 16)
            gate_write(sp, 0, 0, 2 * GROUP)
            gate_read(sp, 0)
            aside = {(-1, 1): lambda: gate_read(sp, 2), (0, 1): lambda: gate_read(sp, 3)}

            def turn(k, slot, has, lap):
                stands_in(aside, k, 0)
                if has(0):
                    wait(sp, mrow_ready, k + 1)
                    sp.dma_start(qs[KQ:KQ + 1, slot(0), :, :, :].rearrange("p h a (t n) -> p (h a t) n", t=TILES),
                                 maxrow[:, slot(0), :]).then_inc(mrow_in, 16)
                if has(2):
                    r = slot(2)
                    wait(sp, parts_out, 16 * (k + 3))
                    for first, q_parts, k_part in ((0, 3, 0), (3, 2, 1), (5, 1, 2)):
                        rows = slice(first * HD, (first + q_parts) * HD)
                        src_q = parts_dram[r, 0:q_parts, 0, :, :].rearrange("s d n -> d s n")
                        src_k = parts_dram[r, k_part, 1, :, :].unsqueeze(1).broadcast_to([HD, q_parts, HEADS * 2 * N])
                        sp.dma_start(qs[rows, r, :, :, :].rearrange("p h a n -> p (h a n)"), src_q).then_inc(stack_in[r], 16)
                        sp.dma_start(ks[rows, r, :, :, :].rearrange("p h a n -> p (h a n)"), src_k).then_inc(stack_in[r], 16)
                stands_in(aside, k, 1)
                if has(3):
                    r = slot(3)
                    wait(sp, split_step, 3 * (k + 4))
                    sp.dma_start(parts_dram[r].rearrange("s g d (h n) -> (g d h) s n", h=HEADS), parts[:, r, :, :]).then_inc(parts_out, 16)
                if has(-2):
                    wait(sp, out_ready, k - 1)
                    if isinstance(k, int):
                        dst = out[2 * (k - 2):2 * (k - 1)].rearrange("i c n -> (i c) n")
                    else:
                        dst = out[bass.ds(2 * (k - 2), 2)].rearrange("i c n -> (i c) n")
                    sp.dma_start(dst, at(xall, k - 2)).then_inc(stored, 16)
            pipeline(sp, turn)
            sp.wait_ge(stored, 16 * PAIRS)

        @block.gpsimd
        def _(pool):
            nc.gpsimd.memset(eps[:, :], EPS).then_inc(eps_ready, 1)
            nc.gpsimd.memset(mhalf[:, :], -0.5).then_inc(mhalf_ready, 1)
            nc.gpsimd.memset(warm[:, :], 0.0).then_inc(warm_ready, 1)
            nc.gpsimd.memset(toep[:, :], 0.0).then_inc(toep_zero, 1)
            pool.wait_ge(mhalf_ready, 1)
            pool.wait_ge(eps_ready, 1)
            pool.wait_ge(rows_in, 16)
            pool.wait_ge(con_in, 16)
            for d in range(KS):
                diagonal = con[:, C_BAND:C_IDENT].rearrange("p (i c) -> p i c", i=2)[:, :, d:d + C]
                nc.gpsimd.tensor_tensor(tapprod[:, d, :].rearrange("p (i c) -> p i c", i=2), diagonal,
                                        wrow[:, d:d + 1].unsqueeze(2).broadcast_to([P, 2, C]), ALU.mult).then_inc(tapprod_ready, 1)
            nc.gpsimd.memset(vs[:, :, :, :, :, :].rearrange("p r t a h d -> p (r t a h) d")[:, :, HD:2 * HD], 1.0).then_inc(fixed_ready, 1)
            pool.wait_ge(fixed_ready, 1)
            nc.gpsimd.memset(ks[KQ:KQ + 1, :, :, :, :], 1.0).then_inc(fixed_ready, 1)
            pool.wait_ge(fixed_ready, 2)
            pool.wait_ge(vec_in, 16)

            def turn(k, slot, has, lap):
                if has(5) and not (isinstance(k, int) and k + 5 in EARLY):
                    if isinstance(k, int) and k + 4 in EARLY:
                        pool.wait_ge(x1_ready, k + 5)
                    for g in [(k + 5) // GROUP] if isinstance(k, int) else range(1, GROUPS):
                        pool.wait_ge(gate_in[g], 32)
                    nc.gpsimd.tensor_tensor(at(ycall, k + 5), at(ycall, k + 5), at(gate, k + 5), ALU.mult).then_inc(u_ready, 1)
                    pool.wait_ge(u_ready, k + 6)
                    nc.gpsimd.tensor_tensor(at(xall, k + 5), at(ycall, k + 5), at(xall, k + 5), ALU.add).then_inc(x1_ready, 1)
                if has(4):
                    wait(pool, gn_mean, k + 5)
                    nc.gpsimd.tensor_tensor(sq[:, :], gmv[:, 0:1], gmv[:, 0:1], ALU.mult).then_inc(sq_ready, 1)
                    wait(pool, sq_ready, k + 5)
                    nc.gpsimd.tensor_tensor(negvar[:, :], sq[:, :], gmv[:, 1:2], ALU.add).then_inc(negvar_ready, 1)
                    wait(pool, negvar_ready, k + 5)
                    nc.gpsimd.tensor_tensor(vareps[:, :], eps[:, :], negvar[:, :], ALU.subtract).then_inc(vareps_ready, 1)
                    wait(pool, vareps_ready, k + 5)
                    nc.gpsimd.tensor_tensor(rstd[:, :], vareps[:, :], mhalf[:, :], ALU.pow).then_inc(rstd_ready, 1)
                on_pool = has(3) and not (isinstance(k, int) and k + 3 == 0)
                if on_pool:
                    r = slot(3)
                    wait(pool, p1_ready, k + 4)
                    wait(pool, z32_ready, k + 4)
                    wait(pool, split_step, 3 * (k + 3))
                    nc.gpsimd.tensor_tensor(rest[:, :], z32[:, :], parts[:, r, 0, :], ALU.subtract).then_inc(split_step, 1)
                    wait(pool, split_step, 3 * (k + 3) + 1)
                if has(4):
                    wait(pool, rstd_ready, k + 5)
                    wait(pool, xn_ready, k + 4)
                    nc.gpsimd.tensor_tensor(gna[:, :], rstd[:, :], w_gn, ALU.mult).then_inc(gn_scale, 1)
                if on_pool:
                    nc.gpsimd.tensor_scalar(parts[:, r, 1, :], rest[:, :], 1.0, 0.0, ALU.mult, ALU.add).then_inc(split_step, 1)
                    wait(pool, split_step, 3 * (k + 3) + 2)
                    nc.gpsimd.tensor_tensor(parts[:, r, 2, :], rest[:, :], parts[:, r, 1, :], ALU.subtract).then_inc(split_step, 1)
                if has(-2) and not (isinstance(k, int) and k - 2 == PAIRS - 1):
                    wait(pool, yo_ready, k - 1)
                    nc.gpsimd.tensor_tensor(at(xall, k - 2), yo[:, slot(-2), :], at(xall, k - 2), ALU.add).then_inc(out_ready, 1)
            pipeline(pool, turn)

        @block.scalar
        def _(act):
            act.wait_ge(mhalf_ready, 1)
            nc.scalar.activation(junk[:, :], mhalf[:, :], ACT.Sigmoid).then_inc(tables_ready, 1)
            def channel_gate(g):
                act.wait_ge(yconv_ready, g + 1)
                nc.scalar.activation(yscale[:, g * GROUP:(g + 1) * GROUP], yconv_bank[g % 2][:, g * GROUP:(g + 1) * GROUP],
                                     ACT.Copy, scale=1.0 / N).then_inc(ys_ready, 1)
                act.wait_ge(ys_ready, g + 1)
                for p in range(g * GROUP, (g + 1) * GROUP):
                    nc.scalar.activation(ycall[:, p, :], xall[:, p, :], ACT.Sigmoid,
                                         scale=yscale[:, p:p + 1]).then_inc(yc_ready, 1)

            def spatial_gate(chunk, images):
                act.wait_ge(sconv_ready, chunk + 1)
                nc.scalar.activation(gate_s[0:images, chunk, :], bank[4][0:images, 0:N], ACT.Sigmoid).then_inc(gate_ready, 1)

            act.wait_ge(ident_in, 16)
            nc.scalar.copy(identb[:, :], ident).then_inc(identb_ready, 1)
            channel_gate(0)
            channel_gate(1)
            spatial_gate(0, 2 * GROUP)
            channel_gate(2)
            channel_gate(3)
            act.wait_ge(pbias_ready, 1)

            def rest_of_gates():
                spatial_gate(1, IMAGES - 2 * GROUP)
                gate_write(act, 1, 2 * GROUP, IMAGES)

            def exp_table():
                act.wait_ge(tables_ready, 1)
                nc.scalar.activation(junk[:, :], mhalf[:, :], ACT.Exp).then_inc(tables_ready, 1)

            aside = {(-2, 3): rest_of_gates, (-1, 0): lambda: gate_read(act, 1), (-1, 3): exp_table}

            def turn(k, slot, has, lap):
                for u in range(UNITS):
                    stands_in(aside, k, u)
                    if u == 0 and has(0):
                        wait(act, mt_ready, k + 1)
                        nc.scalar.copy(maxrow[:, slot(0), :], mt_psum).then_inc(mrow_ready, 1)
                    if u == 5 and has(4):
                        wait(act, gn_shift, k + 5)
                        nc.scalar.activation(xn[:, slot(4), :], at(xall, k + 4), ACT.Identity, bias=gnb[:, 0:1], scale=gna[:, 0:1]).then_inc(xn_ready, 1)
                    if has(-1 if u < LEAD else 0):
                        wait(act, st_ready, UNITS * k + u - LEAD + 1)
                        if u == 0:
                            wait(act, pv_done, 2 * (k - 1))
                        if u == LEAD:
                            wait(act, pv_done, 2 * k - 1)
                        nc.scalar.activation(pt[:, (u + LEAD) % UNITS, :, :].rearrange("p t n -> p (t n)"), st_bank[u % 2][:, :],
                                             ACT.Exp, scale=SCALE).then_inc(exp_done, 1)
                    if u == 0 and has(3):
                        wait(act, z_ready, k + 4)
                        wait(act, parts_out, 16 * k)
                        nc.scalar.activation(parts[:, slot(3), 0, :], z_bank[:, :], ACT.Identity, bias=b_qk).then_inc(p1_ready, 1)
                    if u == 1 and has(3):
                        wait(act, split_step, 3 * (k + 2) + 1)
                        nc.scalar.activation(z32[:, :], z_bank[:, :], ACT.Identity, bias=b_qk).then_inc(z32_ready, 1)
                    if u == 2 and has(1):
                        wait(act, v_ready, k + 2)
                        nc.scalar.copy(vs[:, slot(1), :, :, :, :].rearrange("p t a h d -> p (t a h) d")[:, :, 0:HD],
                                       v_psum.rearrange("p (g d) -> p g d", d=HD)).then_inc(vs_ready, 1)
                    if u == 4 and has(-2) and not (isinstance(k, int) and k - 2 == PAIRS - 1):
                        wait(act, y_ready, k - 1)
                        if not has(3):
                            wait(act, out_ready, k - 5)
                        nc.scalar.activation(yo[:, slot(-2), :], y_psum, ACT.Identity, bias=pbias[:, 0:1]).then_inc(yo_ready, 1)
            pipeline(act, turn)

        @block.vector
        def _(dve):
            dve.wait_ge(rows_in, 16)
            dve.wait_ge(con_in, 16)
            rows = 2 * KS
            dx_mask = con[:, C_DX:C_DX + SIDE * KS].rearrange("p (x d) -> p x d", d=KS).unsqueeze(1).broadcast_to([P, rows, SIDE, KS])
            dx_w = wrow[:, KS:KS + rows * KS].rearrange("p (r d) -> p r d", d=KS).unsqueeze(2).broadcast_to([P, rows, SIDE, KS])
            nc.vector.tensor_tensor(bandprod[:, :].rearrange("p (r x d) -> p r x d", r=rows, d=KS), dx_mask, dx_w,
                                    ALU.mult).then_inc(prod_ready, 1)
            dve.wait_ge(prod_ready, 1)
            nc.vector.tensor_reduce(bandrow[:, 0, :, :].rearrange("p m n -> p (m n)"),
                                    bandprod[:, :].rearrange("p (n d) -> p n d", d=KS), AX.X, ALU.add).then_inc(band_ready, 1)
            dve.wait_ge(band_ready, 1)
            nc.vector.tensor_copy(bandrow[:, 1, :, :], bandrow[:, 0, :, :]).then_inc(band_ready, 1)
            dve.wait_ge(tapprod_ready, KS)
            nc.vector.tensor_reduce(band[:, :], tapprod[:, :, :].rearrange("p d c -> p c d"), AX.X, ALU.add).then_inc(tap_ready, 1)

            def ysums(g):
                dve.wait_ge(x_in[g], 16)
                nc.vector.tensor_reduce(ysum[:, g * GROUP:(g + 1) * GROUP], xall[:, g * GROUP:(g + 1) * GROUP, :],
                                        AX.X, ALU.add).then_inc(ysum_ready, 1)

            def channel_maps(first, last):
                for p in range(first, last):
                    dve.wait_ge(yt_ready, p + 1)
                    product = bank[p % 4][:, 0:2 * (P + 2)].rearrange("p (t n) -> p t n", t=TILES)
                    nc.vector.tensor_reduce(maps[:, :, 1, 2 * p:2 * p + 2],
                                            product[:, :, 0:P].rearrange("p t (i c) -> p t i c", c=C),
                                            AX.X, ALU.max).then_inc(maps_done, 1)
                    nc.vector.tensor_copy(maps[:, :, 0, 2 * p:2 * p + 2], product[:, :, P:P + 2]).then_inc(maps_done, 1)

            def early_x1(p):
                dve.wait_ge(spread_ready, EARLY.index(p) + 1)
                if p == GROUP:
                    dve.wait_ge(x1_ready, p)
                nc.vector.tensor_tensor(ycall[:, p, :], ycall[:, p, :], gate_bank[p][:, 0:N], ALU.mult).then_inc(u_ready, 1)
                dve.wait_ge(u_ready, p + 1)
                nc.vector.tensor_tensor(xall[:, p, :], ycall[:, p, :], xall[:, p, :], ALU.add).then_inc(x1_ready, 1)

            aside = {(-5, 0): lambda: early_x1(0), (-4, 0): lambda: early_x1(1), (-4, 7): lambda: channel_maps(4, 8),
                     (-3, 2): lambda: channel_maps(8, 10), (-3, 3): lambda: channel_maps(10, 12),
                     (-3, 7): lambda: channel_maps(12, 16), (-1, 0): lambda: early_x1(GROUP)}
            ysums(0)
            ysums(1)
            channel_maps(0, GROUP)
            ysums(2)
            ysums(3)
            dve.wait_ge(pb_ready, 1)
            dve.wait_ge(vec_in, 16)
            nc.vector.tensor_tensor(pbias[:, :], bank[5][:, 0:1], b_p, ALU.add).then_inc(pbias_ready, 1)

            def turn(k, slot, has, lap):
                def last(d):
                    return isinstance(k, int) and k + d == PAIRS - 1

                def gn_stats(i):
                    p = k + 5
                    if i == 0:
                        wait(dve, x1_ready, p + 1)
                        op = nc.vector.bn_stats(bn6[:, :], at(xall, p))
                    elif i == 1:
                        op = nc.vector.bn_aggr(mv[:, :], bn6[:, :])
                    else:
                        wait(dve, gn_stat, 3 * p + 2)
                        op = nc.vector.scalar_tensor_tensor(mv[:, 1:2], mv[:, 0:1], mv[:, 0:1], mv[:, 1:2], ALU.mult, ALU.add)
                    op.then_inc(gn_stat, 1)

                def gn_group():
                    wait(dve, gs_ready, k + 5)
                    wait(dve, gn_shift, k + 4)
                    nc.vector.tensor_scalar(gmv[:, :], gs_psum, -1.0, None, ALU.mult).then_inc(gn_mean, 1)

                def gn_shifts():
                    wait(dve, gn_scale, k + 5)
                    nc.vector.scalar_tensor_tensor(gnb[:, :], gmv[:, 0:1], gna[:, 0:1], b_gn, ALU.mult, ALU.add).then_inc(gn_shift, 1)

                def norm(i, d, image=None):
                    steps, sums = 4 * (k + d), 2 * (k + d + 1)
                    cols, blocks = slice(0, 2 * N), slice(0, 2 * N // 32)
                    if image is not None:
                        steps, sums = steps + 4 * image, sums - 1 + image
                        cols, blocks = slice(image * N, (image + 1) * N), slice(image * N // 32, (image + 1) * N // 32)
                    if i == 0:
                        wait(dve, pv_done, sums)
                        if image == 0:
                            dve.wait_ge(norm_step, steps)
                        op = nc.vector.transpose(o_tok[:, blocks, :].rearrange("p b c -> p (b c)"), o_bank[:, cols])
                    else:
                        wait(dve, norm_step, steps + i)
                        if i == 1:
                            op = nc.vector.reciprocal(orec[:, blocks], o_tok[:, blocks, HD])
                        elif i == 2:
                            op = nc.vector.tensor_tensor(o_tok[:, blocks, 0:HD], o_tok[:, blocks, 0:HD],
                                                         orec[:, blocks].unsqueeze(2).broadcast_to([P, blocks.stop - blocks.start, HD]), ALU.mult)
                        else:
                            if image == 0:
                                dve.wait_ge(y_ready, k + d)
                            op = nc.vector.transpose(onorm[:, cols], o_tok[:, blocks, :].rearrange("p b c -> p (b c)"))
                    op.then_inc(norm_step, 1)

                for u in range(UNITS):
                    stands_in(aside, k, u)
                    if has(1):
                        wait(dve, s_ready, UNITS * (k + 1) + u + 1)
                        nc.vector.tensor_reduce(negmax[:, slot(1), u % HEADS, u // HEADS, :],
                                                s_bank[u % 2][:, :].rearrange("p (t n) -> p t n", t=TILES),
                                                AX.X, ALU.max, negate=True).then_inc(max_done, 1)
                    if u == 0 and has(4):
                        gn_group()
                    if u <= 2 and has(-2):
                        norm(u + 1, -2, 1 if last(-2) else None)
                    if u == 2 and isinstance(k, int) and k + 3 == 0:
                        dve.wait_ge(p1_ready, 1)
                        dve.wait_ge(z32_ready, 1)
                        nc.vector.tensor_tensor(rest[:, :], z32[:, :], parts[:, 0, 0, :], ALU.subtract).then_inc(split_step, 1)
                        dve.wait_ge(split_step, 1)
                        nc.vector.tensor_copy(parts[:, 0, 1, :], rest[:, :]).then_inc(split_step, 1)
                        dve.wait_ge(split_step, 2)
                        nc.vector.tensor_tensor(parts[:, 0, 2, :], rest[:, :], parts[:, 0, 1, :], ALU.subtract).then_inc(split_step, 1)
                    if u == 3 and has(5):
                        gn_stats(0)
                    if u == 4:
                        if has(5):
                            wait(dve, gn_stat, 3 * (k + 5) + 1)
                        if has(4):
                            gn_shifts()
                        if has(5):
                            gn_stats(1)
                    if u == 5 and has(5):
                        gn_stats(2)
                    if u == 4 and last(-1):
                        for i in range(4):
                            norm(i, -1, 0)
                    if u == 7 and has(-1):
                        norm(0, -1, 1 if last(-1) else None)
                    if u == 4 and last(-2):
                        dve.wait_ge(y_ready, PAIRS)
                        dve.wait_ge(out_ready, PAIRS - 1)
                        nc.vector.scalar_tensor_tensor(xall[:, PAIRS - 1, :], y_psum, pbias[:, 0:1], xall[:, PAIRS - 1, :],
                                                       ALU.add, ALU.add).then_inc(out_ready, 1)
            pipeline(dve, turn)

        @block.tensor
        def _(pe):
            def keep_busy(count, bank=bank[3]):
                for _ in range(count):
                    pe.matmul(bank[:, :], warm[:, 0:P], warm[:, :], start=True, stop=True)

            pe.wait_ge(warm_ready, 1)
            keep_busy(18, bank[5])

            def channel_conv(g):
                pe.wait_ge(ysum_ready, g + 1)
                if g >= 2:
                    pe.wait_ge(ys_ready, g - 1)
                pe.matmul(yconv_bank[g % 2][:, g * GROUP:(g + 1) * GROUP], band[:, :], ysum[:, g * GROUP:(g + 1) * GROUP],
                          start=True, stop=True).then_inc(yconv_ready, 1)

            def transposes(g):
                for p in range(g * GROUP, (g + 1) * GROUP):
                    pe.wait_ge(yc_ready, p + 1)
                    if p >= 4:
                        pe.wait_ge(maps_done, 2 * (p - 3))
                    if p == 6:
                        pe.wait_ge(ys_ready, 3)
                    if p == 7:
                        pe.wait_ge(u_ready, 1)
                    for t in range(TILES):
                        mm = pe.matmul(bank[p % 4][:, t * (P + 2):(t + 1) * (P + 2)], ycall[:, p, t * P:(t + 1) * P],
                                       con[:, C_IDENT:C_GROUP], start=True, stop=True)
                    mm.then_inc(yt_ready, 1)

            def spatial_conv(chunk, first, last):
                pe.wait_ge(maps_done, last)
                for t in range(TILES):
                    for m in range(2):
                        c = (2 * t + m) * TSTRIDE - t * P + KS // 2 * SIDE
                        mm = pe.matmul(bank[4][0:last - first, 0:N], maps[:, t, m, first:last], toep[:, c:c + N],
                                       start=(t == 0 and m == 0), stop=(t == TILES - 1 and m == 1))
                mm.then_inc(sconv_ready, 1)

            def spread_gate(p, chunk):
                pe.wait_ge(gate_ready, chunk + 1)
                pe.wait_ge(sel_in, 16)
                first = p % GROUP * P
                pe.matmul(gate_bank[p][:, 0:N], sel[:, first:first + P], gate_s[0:2 * GROUP, chunk, :],
                          start=True, stop=True).then_inc(spread_ready, 1)

            def transposes_2_3():
                transposes(2)
                transposes(3)

            aside = {(-5, 0): lambda: transposes(1), (-4, 0): lambda: keep_busy(8, bank[5]), (-3, 2): transposes_2_3,
                     (-2, 2): lambda: spatial_conv(1, 2 * GROUP, IMAGES), (-2, 3): lambda: keep_busy(4),
                     (-2, 4): lambda: spread_gate(GROUP, 1), (-1, 0): lambda: keep_busy(3)}
            aside.update({(-1, u): lambda: keep_busy(2) for u in range(1, UNITS)})
            aside.update({(0, u): lambda: keep_busy(1, bank[4]) for u in range(UNITS)})
            pe.wait_ge(tap_ready, 1)
            channel_conv(0)
            pe.wait_ge(ident_in, 16)
            keep_busy(2, bank[5])
            channel_conv(1)
            keep_busy(3, bank[5])
            transposes(0)
            pe.wait_ge(toep_in, 16 * SIDE // TILES)
            spatial_conv(0, 0, 2 * GROUP)
            channel_conv(2)
            channel_conv(3)
            pe.wait_ge(wall_in, 16)
            pe.wait_ge(vec_in, 16)
            for a in range(2):
                mm = pe.matmul(bank[5][64 * a:64 * a + 64, 0:1], w_p, b_v, start=True, stop=True)
            mm.then_inc(pb_ready, 1)
            spread_gate(0, 0)
            spread_gate(1, 0)
            pe.wait_ge(identb_ready, 1)
            pe.wait_ge(fixed_ready, 2)
            pe.wait_ge(pbias_ready, 1)

            def turn(k, slot, has, lap):
                def s(u):
                    a, h = u // HEADS, u % HEADS
                    wait(pe, max_done, UNITS * (k + 1) + u - 1)
                    if u == 0:
                        wait(pe, stack_in[slot(1)], lap(1) * 96)
                    for t in range(TILES):
                        mm = pe.matmul(s_bank[u % 2][:, t * N:(t + 1) * N], qs[0:KQ, slot(1), h, a, t * P:(t + 1) * P],
                                       ks[0:KQ, slot(1), h, a, :], start=True, stop=True)
                    mm.then_inc(s_ready, 1)

                def st(u):
                    d, unit = (-1, u + LEAD) if u < LEAD else (0, u - LEAD)
                    a, h = unit // HEADS, unit % HEADS
                    wait(pe, exp_done, UNITS * k + u - LEAD - 1)
                    if unit == 0:
                        wait(pe, mrow_in, 16 * (k + 1))
                    for t in range(TILES):
                        mm = pe.matmul(st_bank[u % 2][:, t * N:(t + 1) * N], ks[0:KQ + 1, slot(d), h, a, t * P:(t + 1) * P],
                                       qs[0:KQ + 1, slot(d), h, a, :], start=True, stop=True)
                    mm.then_inc(st_ready, 1)

                def pv(a, t):
                    if t == 0:
                        wait(pe, exp_done, UNITS * (k - 1) + HEADS * (a + 1))
                        if a == 1 and isinstance(k, int) and k == PAIRS:
                            pe.wait_ge(norm_step, 4 * (k - 1) + 1)
                        if a == 0:
                            wait(pe, norm_step, 4 * (k - 2) + 1)
                            wait(pe, vs_ready, k)
                    for h in range(HEADS):
                        mm = pe.matmul(o_bank[32 * h:32 * h + 32, a * N:(a + 1) * N], vs[:, slot(-1), t, a, h, :],
                                       pt[:, HEADS * a + h, t, :], start=(t == 0), stop=(t == TILES - 1))
                    if t == TILES - 1:
                        mm.then_inc(pv_done, 1)

                def qk(a):
                    d = 4 - a
                    if a == 0:
                        wait(pe, xn_ready, k + 5)
                        wait(pe, z32_ready, k + 4)
                    mm = pe.matmul(z_bank[:, a * N:(a + 1) * N], w_qk[a], xn[:, slot(d), :], start=True, stop=True)
                    if a == 1:
                        mm.then_inc(z_ready, 1)

                def v():
                    wait(pe, mrow_ready, k + 1)
                    for t in range(TILES):
                        mm = pe.matmul(v_psum[:, t * P:(t + 1) * P], xn[:, slot(1), t * P:(t + 1) * P], w_v, start=True, stop=True)
                    mm.then_inc(v_ready, 1)

                def proj():
                    wait(pe, norm_step, 4 * PAIRS + 4 if isinstance(k, int) and k == PAIRS + 1 else 4 * (k - 1))
                    if has(4):
                        wait(pe, gn_mean, k + 5)
                    else:
                        wait(pe, yo_ready, k - 2)
                    for a in range(2):
                        mm = pe.matmul(y_psum[64 * a:64 * a + 64, :], w_p, onorm[:, a * N:(a + 1) * N], start=True, stop=True)
                    mm.then_inc(y_ready, 1)

                def groupstats():
                    wait(pe, gn_stat, 3 * (k + 6))
                    wait(pe, gn_mean, k + 5)
                    wait(pe, yo_ready, k - 1)
                    mm = pe.matmul(gs_psum, groupavg, mv[:, :], start=True, stop=True)
                    mm.then_inc(gs_ready, 1)

                def maxt():
                    wait(pe, max_done, UNITS * (k + 1))
                    wait(pe, vs_ready, k + 1)
                    mm = pe.transpose(mt_psum, negmax[:, slot(0), :, :, :].rearrange("p h a t -> p (h a t)"), identb[:, :])
                    mm.then_inc(mt_ready, 1)

                for u in range(UNITS):
                    stands_in(aside, k, u)
                    if has(1):
                        s(u)
                    if has(-1 if u < LEAD else 0):
                        st(u)
                    if u == 0 and has(0):
                        maxt()
                    if u == 0 and has(3):
                        qk(1)
                    if u == 1 and has(1):
                        v()
                    if u in (2, 3) and has(-1):
                        pv(0, u - 2)
                    if u == 4 and has(-2):
                        proj()
                    if u in (5, 6) and has(-1):
                        pv(1, u - 5)
                    if u == 7 and has(5):
                        groupstats()
                    if u == 7 and has(4):
                        qk(0)
            pipeline(pe, turn)


def constants():
    import numpy as np
    c = np.zeros((P, C_END), np.float32)
    i, j = np.arange(P)[:, None], np.arange(P)[None, :]
    c[:, C_IDENT:C_IDENT + P] = i == j
    for r in range(P):
        c[r, C_BAND + r // C * PADC + r % C + KS // 2] = 1
    xp, d = np.arange(SIDE)[:, None], np.arange(KS)[None, :]
    for r in range(P):
        c[r, C_DX:C_DX + SIDE * KS] = (r % SIDE - xp + KS // 2 == d).reshape(-1)
    c[:, C_GROUP:C_GROUP + P] = 0.5 * (i // 2 == j // 2)
    c[:, C_MEAN:C_MEAN + 2] = (i // C == np.arange(2)[None, :]) / C
    sel = (np.arange(2 * GROUP)[:, None] == np.arange(2 * P)[None, :] // C).astype(np.float32)
    return c, sel


def kernel(x, L0_conv_w_c, L0_conv_w_s, L1_conv_gn_w, L1_conv_gn_b, L1_conv_qkv_w, L1_conv_qkv_b, L1_conv_proj_w, L1_conv_proj_b):
    import numpy as np
    import concourse.bacc as bacc
    from concourse.bass_utils import run_bass_kernel_spmd

    x, w_c, w_s, gn_w, gn_b, qkv_w, qkv_b, proj_w, proj_b = (np.asarray(a) for a in (
        x, L0_conv_w_c, L0_conv_w_s, L1_conv_gn_w, L1_conv_gn_b, L1_conv_qkv_w, L1_conv_qkv_b, L1_conv_proj_w, L1_conv_proj_b))
    w_rows = np.concatenate([w_c.reshape(-1), w_s[0, :, ::-1, :].reshape(-1)])
    qk = qkv_w[:2 * C].reshape(2, HEADS, HD, C).transpose(3, 0, 2, 1).reshape(C, 2 * C)
    w_all = np.zeros((P, 448), np.float32)
    w_all[0:C, 0:128] = qk
    w_all[C:P, 128:256] = qk
    w_all[0:C, 256:320] = qkv_w[2 * C:].T
    w_all[C:P, 320:384] = qkv_w[2 * C:].T
    vecs = np.zeros((P, 5), np.float32)
    vecs[:, 0] = qkv_b[:2 * C].reshape(2, HEADS, HD).transpose(0, 2, 1).reshape(-1)
    for h in range(HEADS):
        w_all[32 * h:32 * h + HD, 384:448] = proj_w[:, h * HD:(h + 1) * HD].T
        vecs[32 * h:32 * h + HD, 1] = qkv_b[2 * C + h * HD:2 * C + (h + 1) * HD]
    for i, v in ((2, proj_b), (3, gn_w), (4, gn_b)):
        vecs[0:C, i] = v
        vecs[C:P, i] = v
    con, sel = constants()
    arrays = {"x": x.reshape(IMAGES, C, N), "w_rows": w_rows, "vecs": vecs, "w_all": w_all, "select": sel, "consts": con}

    nc = bacc.Bacc("TRN2", target_bir_lowering=False, num_devices=1)
    args = [nc.dram_tensor(n, list(a.shape), F32, kind="ExternalInput").ap() for n, a in arrays.items()]
    out = nc.dram_tensor("out", [IMAGES, C, N], F32, kind="ExternalOutput").ap()
    program(nc, *args, out)
    r = run_bass_kernel_spmd(nc, [{n: np.ascontiguousarray(a) for n, a in arrays.items()}], core_ids=[0])
    return r.results[0]["out"].reshape(IMAGES, C, SIDE, SIDE)
```
